# Optimizing a Trainium2 kernel written in Bass

```python
import numpy as np
import jax
import jax.numpy as jnp

def _softmax(x, axis=-1):
    return jax.nn.softmax(x, axis=axis)

def _gelu(x):
    return jax.nn.gelu(x, approximate=True)

def _silu(x):
    return jax.nn.silu(x)

def _sigmoid(x):
    return jax.nn.sigmoid(x)

def _layernorm(x, axis=-1, eps=1e-05):
    m = jnp.mean(x, axis=axis, keepdims=True)
    v = jnp.var(x, axis=axis, keepdims=True)
    return (x - m) / jnp.sqrt(v + eps)

def _scatter_add(tgt, idx, src, axis=0):
    return tgt.at[idx].add(src)

def _segment_sum(src, seg, n):
    return jax.ops.segment_sum(src, seg, n)
kernel_name = 'mk_xattn_seq_d4_seqx_r8_51b3aa'

def setup_inputs(seed: int=0):
    np.random.seed(seed)
    _w = jnp.asarray

    def _rec_inputs():
        import jax
        import jax.numpy as jnp
        _rk = jax.random.key(seed)
        x = -0.0002928 + 1 * jax.random.normal(jax.random.fold_in(_rk, 1), (64, 64, 128), jnp.float32)
        _lenS = 64 - jax.random.randint(jax.random.fold_in(_rk, 7), (64,), 0, max(1, 64 // 4) + 1, jnp.int32)
        _lenS2 = 64 - jax.random.randint(jax.random.fold_in(_rk, 8), (64,), 0, max(1, 64 // 4) + 1, jnp.int32)
        _ctx_1024P = jax.random.normal(jax.random.fold_in(_rk, 11), (64, 16, 128), jnp.float32)
        _ctx_1024c = jax.random.dirichlet(jax.random.fold_in(_rk, 511), 0.3 * jnp.ones((16,), jnp.float32), (64, 64))
        _ctx_1024t = jnp.einsum('bsk,bkd->bsd', _ctx_1024c, _ctx_1024P)
        _ctx_1024t = _ctx_1024t * jax.lax.rsqrt(jnp.mean(jnp.square(_ctx_1024t)) + 1e-12) * 0.953939
        ctx_1024 = -1.39393e-06 + 0.999914 * (_ctx_1024t + 0.3 * jax.random.normal(jax.random.fold_in(_rk, 611), (64, 64, 128), jnp.float32))
        return (x, ctx_1024)
    x, ctx_1024 = _rec_inputs()

    def _L0_xattn_setup():
        import jax, jax.numpy as jnp
        import numpy as np
        EPS = 1e-05

        def _layernorm(x, g, b):
            m = jnp.mean(x, axis=-1, keepdims=True)
            v = jnp.mean((x - m) ** 2, axis=-1, keepdims=True)
            return (x - m) / jnp.sqrt(v + EPS) * g + b

        def _mha(x, kv, Wq, Wk, Wv, mask, causal):
            m = mask[:, None]
            Q = jnp.einsum('bsd,hdk->bhsk', x, Wq) * m
            K = jnp.einsum('bsd,hdk->bhsk', kv, Wk) * m
            V = jnp.einsum('bsd,hdk->bhsk', kv, Wv) * m
            energy = jnp.einsum('bhsk,bhtk->bhst', Q, K)
            S = energy.shape[-1]
            lengths = jnp.sum(energy[:, :, 0, :] != 0, axis=-1)
            cols = jnp.arange(S)
            energy = jnp.where(cols[None, None, None, :] >= lengths[:, :, None, None], -jnp.inf, energy)
            if causal:
                energy = jnp.where(cols[None, :] > cols[:, None], -jnp.inf, energy)
            dk = Wq.shape[-1]
            score = jax.nn.softmax(energy / jnp.sqrt(jnp.asarray(dk, energy.dtype)), axis=-1)
            out = jnp.einsum('bhst,bhtk->bhsk', score, V) * m
            B, H, Sx, dkk = out.shape
            return out.transpose(0, 2, 1, 3).reshape(B, Sx, H * dkk)
        key = jax.random.key(seed)
        ks = jax.random.split(key, 20)
        B, S, D, H = (2, 256, 128, 16)
        dk = D // H
        sd = 0.02
        inp = {'x': jax.random.normal(ks[0], (B, S, D), jnp.float32), 'context': jax.random.normal(ks[1], (B, S, D), jnp.float32), 'Wq1': jax.random.normal(ks[2], (H, D, dk), jnp.float32) * sd, 'Wk1': jax.random.normal(ks[3], (H, D, dk), jnp.float32) * sd, 'Wv1': jax.random.normal(ks[4], (H, D, dk), jnp.float32) * sd, 'Wq2': jax.random.normal(ks[5], (H, D, dk), jnp.float32) * sd, 'Wk2': jax.random.normal(ks[6], (H, D, dk), jnp.float32) * sd, 'Wv2': jax.random.normal(ks[7], (H, D, dk), jnp.float32) * sd, 'ln1_g': jnp.ones((D,), jnp.float32), 'ln1_b': jnp.zeros((D,), jnp.float32), 'ln2_g': jnp.ones((D,), jnp.float32), 'ln2_b': jnp.zeros((D,), jnp.float32), 'ln3_g': jnp.ones((D,), jnp.float32), 'ln3_b': jnp.zeros((D,), jnp.float32), 'fc1_w': jax.random.normal(ks[8], (D, D), jnp.float32) * sd, 'fc1_b': jnp.zeros((D,), jnp.float32), 'fc2_w': jax.random.normal(ks[9], (D, D), jnp.float32) * sd, 'fc2_b': jnp.zeros((D,), jnp.float32)}
        return inp
    _L0_xattn_all = _L0_xattn_setup()
    _L0_xattn_in = {k: v for k, v in _L0_xattn_all.items() if k in ('Wq1', 'Wk1', 'Wv1', 'Wq2', 'Wk2', 'Wv2', 'ln1_g', 'ln1_b', 'ln2_g', 'ln2_b', 'ln3_g', 'ln3_b', 'fc1_w', 'fc1_b', 'fc2_w', 'fc2_b')}
    del _L0_xattn_all

    def _L1_xattn_setup():
        import jax, jax.numpy as jnp
        import numpy as np
        D = 128
        H = 16
        HD = D // H
        DFF = 4 * D
        LN_EPS = 1e-05

        def layernorm(x, gamma, beta):
            mu = jnp.mean(x, axis=-1, keepdims=True)
            var = jnp.mean(jnp.square(x - mu), axis=-1, keepdims=True)
            return (x - mu) * jax.lax.rsqrt(var + LN_EPS) * gamma + beta
        key = jax.random.key(seed)
        ks = jax.random.split(key, 10)
        B, Nq, Nk = (2, 256, 256)
        s = 0.02
        return {'q_x': jax.random.normal(ks[0], (B, Nq, D), jnp.float32), 'kv_x': jax.random.normal(ks[1], (B, Nk, D), jnp.float32), 'Wq': jax.random.normal(ks[2], (D, D), jnp.float32) * s, 'Wkv': jax.random.normal(ks[3], (2 * D, D), jnp.float32) * s, 'Wo': jax.random.normal(ks[4], (D, D), jnp.float32) * s, 'bo': jnp.zeros((D,), jnp.float32), 'ln_q_g': jnp.ones((D,), jnp.float32), 'ln_q_b': jnp.zeros((D,), jnp.float32), 'ln_kv_g': jnp.ones((D,), jnp.float32), 'ln_kv_b': jnp.zeros((D,), jnp.float32), 'W1': jax.random.normal(ks[5], (DFF, D), jnp.float32) * s, 'b1': jnp.zeros((DFF,), jnp.float32), 'W2': jax.random.normal(ks[6], (D, DFF), jnp.float32) * s, 'b2': jnp.zeros((D,), jnp.float32)}
    _L1_xattn_all = _L1_xattn_setup()
    _L1_xattn_in = {k: v for k, v in _L1_xattn_all.items() if k in ('Wq', 'Wkv', 'Wo', 'bo', 'ln_q_g', 'ln_q_b', 'ln_kv_g', 'ln_kv_b', 'W1', 'b1', 'W2', 'b2')}
    del _L1_xattn_all

    def _L2_xattn_setup():
        import jax, jax.numpy as jnp
        import numpy as np
        B, S, D, H, FF = (2, 256, 128, 16, 512)
        DK = D // H
        LN_EPS = 1e-05

        def layer_norm(x, g, b):
            mu = jnp.mean(x, axis=-1, keepdims=True)
            var = jnp.var(x, axis=-1, keepdims=True)
            return (x - mu) * jax.lax.rsqrt(var + LN_EPS) * g + b

        def split_heads(t):
            b, l, _ = t.shape
            return t.reshape(b, l, H, DK).transpose(0, 2, 1, 3)

        def mha(q_in, k_in, v_in, wq, wk, wv, wo, causal):
            q = split_heads(q_in @ wq)
            k = split_heads(k_in @ wk)
            v = split_heads(v_in @ wv)
            attn = jnp.einsum('bhqd,bhkd->bhqk', q, k) * DK ** (-0.5)
            if causal:
                lq = q.shape[2]
                mask = jnp.tril(jnp.ones((lq, lq), dtype=bool))
                attn = jnp.where(mask, attn, -jnp.inf)
            attn = jax.nn.softmax(attn, axis=-1)
            out = jnp.einsum('bhqk,bhkd->bhqd', attn, v)
            out = out.transpose(0, 2, 1, 3).reshape(q_in.shape[0], q_in.shape[1], D)
            return out @ wo
        key = jax.random.key(seed)
        ks = jax.random.split(key, 16)
        s = 1.0 / np.sqrt(D)
        inp = {'x': jax.random.normal(ks[0], (B, S, D), jnp.float32), 'encoder_output': jax.random.normal(ks[1], (B, S, D), jnp.float32), 'sa_wq': jax.random.normal(ks[2], (D, D), jnp.float32) * s, 'sa_wk': jax.random.normal(ks[3], (D, D), jnp.float32) * s, 'sa_wv': jax.random.normal(ks[4], (D, D), jnp.float32) * s, 'sa_wo': jax.random.normal(ks[5], (D, D), jnp.float32) * s, 'ca_wq': jax.random.normal(ks[6], (D, D), jnp.float32) * s, 'ca_wk': jax.random.normal(ks[7], (D, D), jnp.float32) * s, 'ca_wv': jax.random.normal(ks[8], (D, D), jnp.float32) * s, 'ca_wo': jax.random.normal(ks[9], (D, D), jnp.float32) * s, 'ffn_w1': jax.random.normal(ks[10], (D, FF), jnp.float32) * s, 'ffn_b1': jnp.zeros((FF,), jnp.float32), 'ffn_w2': jax.random.normal(ks[11], (FF, D), jnp.float32) * (1.0 / np.sqrt(FF)), 'ffn_b2': jnp.zeros((D,), jnp.float32), 'ln1_g': jnp.ones((D,), jnp.float32), 'ln1_b': jnp.zeros((D,), jnp.float32), 'ln2_g': jnp.ones((D,), jnp.float32), 'ln2_b': jnp.zeros((D,), jnp.float32), 'ln3_g': jnp.ones((D,), jnp.float32), 'ln3_b': jnp.zeros((D,), jnp.float32)}
        return inp
    _L2_xattn_all = _L2_xattn_setup()
    _L2_xattn_in = {k: v for k, v in _L2_xattn_all.items() if k in ('sa_wq', 'sa_wk', 'sa_wv', 'sa_wo', 'ca_wq', 'ca_wk', 'ca_wv', 'ca_wo', 'ffn_w1', 'ffn_b1', 'ffn_w2', 'ffn_b2', 'ln1_g', 'ln1_b', 'ln2_g', 'ln2_b', 'ln3_g', 'ln3_b')}
    del _L2_xattn_all

    def _L3_xattn_setup():
        import jax, jax.numpy as jnp
        import numpy as np
        NEG = -4294967295.0
        EPS = 1e-08
        H = 4
        L = 3

        def _layer_norm(x, g, b):
            mean = jnp.mean(x, axis=-1, keepdims=True)
            std = jnp.std(x, axis=-1, keepdims=True, ddof=1)
            return g * (x - mean) / (std + EPS) + b

        def _mha_layer(q, k, v, Wq, bq, Wk, bk, Wv, bv, gamma, beta):
            B, Sq, d = q.shape
            Sk = k.shape[1]
            dh = d // H
            Q = jax.nn.relu(q @ Wq + bq)
            K = jax.nn.relu(k @ Wk + bk)
            V = jax.nn.relu(v @ Wv + bv)
            Qh = Q.reshape(B, Sq, H, dh).transpose(2, 0, 1, 3)
            Kh = K.reshape(B, Sk, H, dh).transpose(2, 0, 1, 3)
            Vh = V.reshape(B, Sk, H, dh).transpose(2, 0, 1, 3)
            scores = jnp.einsum('hbqd,hbkd->hbqk', Qh, Kh) / jnp.sqrt(jnp.float32(dh))
            key_mask = jnp.sign(jnp.abs(jnp.sum(k, axis=-1)))
            scores = jnp.where(key_mask[None, :, None, :] == 0.0, NEG, scores)
            attn = jax.nn.softmax(scores, axis=-1)
            query_mask = jnp.sign(jnp.abs(jnp.sum(q, axis=-1)))
            attn = attn * query_mask[None, :, :, None]
            out = jnp.einsum('hbqk,hbkd->hbqd', attn, Vh)
            out = out.transpose(1, 2, 0, 3).reshape(B, Sq, d)
            out = out + q
            return _layer_norm(out, gamma, beta)
        key = jax.random.key(seed)
        ks = jax.random.split(key, 8)
        B, S, d = (2, 256, 128)
        inp = {'queries': jax.random.normal(ks[0], (B, S, d), jnp.float32), 'keys': jax.random.normal(ks[1], (B, S, d), jnp.float32), 'values': jax.random.normal(ks[2], (B, S, d), jnp.float32), 'Wq': jax.random.normal(ks[3], (L, d, d), jnp.float32) * 0.02, 'bq': jnp.zeros((L, d), jnp.float32), 'Wk': jax.random.normal(ks[4], (L, d, d), jnp.float32) * 0.02, 'bk': jnp.zeros((L, d), jnp.float32), 'Wv': jax.random.normal(ks[5], (L, d, d), jnp.float32) * 0.02, 'bv': jnp.zeros((L, d), jnp.float32), 'gamma': jnp.ones((L, d), jnp.float32), 'beta': jnp.zeros((L, d), jnp.float32), 'Wff': jax.random.normal(ks[6], (L, d, d), jnp.float32) * 0.02, 'bff': jnp.zeros((L, d), jnp.float32)}
        return inp
    _L3_xattn_all = _L3_xattn_setup()
    _L3_xattn_in = {k: v for k, v in _L3_xattn_all.items() if k in ('Wq', 'bq', 'Wk', 'bk', 'Wv', 'bv', 'gamma', 'beta', 'Wff', 'bff')}
    del _L3_xattn_all
    return {'x': x, 'ctx_1024': ctx_1024, 'L0_xattn_Wq1': _L0_xattn_in['Wq1'], 'L0_xattn_Wk1': _L0_xattn_in['Wk1'], 'L0_xattn_Wv1': _L0_xattn_in['Wv1'], 'L0_xattn_Wq2': _L0_xattn_in['Wq2'], 'L0_xattn_Wk2': _L0_xattn_in['Wk2'], 'L0_xattn_Wv2': _L0_xattn_in['Wv2'], 'L0_xattn_ln1_g': _L0_xattn_in['ln1_g'], 'L0_xattn_ln1_b': _L0_xattn_in['ln1_b'], 'L0_xattn_ln2_g': _L0_xattn_in['ln2_g'], 'L0_xattn_ln2_b': _L0_xattn_in['ln2_b'], 'L0_xattn_ln3_g': _L0_xattn_in['ln3_g'], 'L0_xattn_ln3_b': _L0_xattn_in['ln3_b'], 'L0_xattn_fc1_w': _L0_xattn_in['fc1_w'], 'L0_xattn_fc1_b': _L0_xattn_in['fc1_b'], 'L0_xattn_fc2_w': _L0_xattn_in['fc2_w'], 'L0_xattn_fc2_b': _L0_xattn_in['fc2_b'], 'L1_xattn_Wq': _L1_xattn_in['Wq'], 'L1_xattn_Wkv': _L1_xattn_in['Wkv'], 'L1_xattn_Wo': _L1_xattn_in['Wo'], 'L1_xattn_bo': _L1_xattn_in['bo'], 'L1_xattn_ln_q_g': _L1_xattn_in['ln_q_g'], 'L1_xattn_ln_q_b': _L1_xattn_in['ln_q_b'], 'L1_xattn_ln_kv_g': _L1_xattn_in['ln_kv_g'], 'L1_xattn_ln_kv_b': _L1_xattn_in['ln_kv_b'], 'L1_xattn_W1': _L1_xattn_in['W1'], 'L1_xattn_b1': _L1_xattn_in['b1'], 'L1_xattn_W2': _L1_xattn_in['W2'], 'L1_xattn_b2': _L1_xattn_in['b2'], 'L2_xattn_sa_wq': _L2_xattn_in['sa_wq'], 'L2_xattn_sa_wk': _L2_xattn_in['sa_wk'], 'L2_xattn_sa_wv': _L2_xattn_in['sa_wv'], 'L2_xattn_sa_wo': _L2_xattn_in['sa_wo'], 'L2_xattn_ca_wq': _L2_xattn_in['ca_wq'], 'L2_xattn_ca_wk': _L2_xattn_in['ca_wk'], 'L2_xattn_ca_wv': _L2_xattn_in['ca_wv'], 'L2_xattn_ca_wo': _L2_xattn_in['ca_wo'], 'L2_xattn_ffn_w1': _L2_xattn_in['ffn_w1'], 'L2_xattn_ffn_b1': _L2_xattn_in['ffn_b1'], 'L2_xattn_ffn_w2': _L2_xattn_in['ffn_w2'], 'L2_xattn_ffn_b2': _L2_xattn_in['ffn_b2'], 'L2_xattn_ln1_g': _L2_xattn_in['ln1_g'], 'L2_xattn_ln1_b': _L2_xattn_in['ln1_b'], 'L2_xattn_ln2_g': _L2_xattn_in['ln2_g'], 'L2_xattn_ln2_b': _L2_xattn_in['ln2_b'], 'L2_xattn_ln3_g': _L2_xattn_in['ln3_g'], 'L2_xattn_ln3_b': _L2_xattn_in['ln3_b'], 'L3_xattn_Wq': _L3_xattn_in['Wq'], 'L3_xattn_bq': _L3_xattn_in['bq'], 'L3_xattn_Wk': _L3_xattn_in['Wk'], 'L3_xattn_bk': _L3_xattn_in['bk'], 'L3_xattn_Wv': _L3_xattn_in['Wv'], 'L3_xattn_bv': _L3_xattn_in['bv'], 'L3_xattn_gamma': _L3_xattn_in['gamma'], 'L3_xattn_beta': _L3_xattn_in['beta'], 'L3_xattn_Wff': _L3_xattn_in['Wff'], 'L3_xattn_bff': _L3_xattn_in['bff']}

def reference(x, ctx_1024, L0_xattn_Wq1, L0_xattn_Wk1, L0_xattn_Wv1, L0_xattn_Wq2, L0_xattn_Wk2, L0_xattn_Wv2, L0_xattn_ln1_g, L0_xattn_ln1_b, L0_xattn_ln2_g, L0_xattn_ln2_b, L0_xattn_ln3_g, L0_xattn_ln3_b, L0_xattn_fc1_w, L0_xattn_fc1_b, L0_xattn_fc2_w, L0_xattn_fc2_b, L1_xattn_Wq, L1_xattn_Wkv, L1_xattn_Wo, L1_xattn_bo, L1_xattn_ln_q_g, L1_xattn_ln_q_b, L1_xattn_ln_kv_g, L1_xattn_ln_kv_b, L1_xattn_W1, L1_xattn_b1, L1_xattn_W2, L1_xattn_b2, L2_xattn_sa_wq, L2_xattn_sa_wk, L2_xattn_sa_wv, L2_xattn_sa_wo, L2_xattn_ca_wq, L2_xattn_ca_wk, L2_xattn_ca_wv, L2_xattn_ca_wo, L2_xattn_ffn_w1, L2_xattn_ffn_b1, L2_xattn_ffn_w2, L2_xattn_ffn_b2, L2_xattn_ln1_g, L2_xattn_ln1_b, L2_xattn_ln2_g, L2_xattn_ln2_b, L2_xattn_ln3_g, L2_xattn_ln3_b, L3_xattn_Wq, L3_xattn_bq, L3_xattn_Wk, L3_xattn_bk, L3_xattn_Wv, L3_xattn_bv, L3_xattn_gamma, L3_xattn_beta, L3_xattn_Wff, L3_xattn_bff):
    import jax
    import jax.numpy as jnp

    def _L0_xattn_ref(x, context, Wq1, Wk1, Wv1, Wq2, Wk2, Wv2, ln1_g, ln1_b, ln2_g, ln2_b, ln3_g, ln3_b, fc1_w, fc1_b, fc2_w, fc2_b):
        import jax, jax.numpy as jnp
        import numpy as np
        EPS = 1e-05

        def _layernorm(x, g, b):
            m = jnp.mean(x, axis=-1, keepdims=True)
            v = jnp.mean((x - m) ** 2, axis=-1, keepdims=True)
            return (x - m) / jnp.sqrt(v + EPS) * g + b

        def _mha(x, kv, Wq, Wk, Wv, mask, causal):
            m = mask[:, None]
            Q = jnp.einsum('bsd,hdk->bhsk', x, Wq) * m
            K = jnp.einsum('bsd,hdk->bhsk', kv, Wk) * m
            V = jnp.einsum('bsd,hdk->bhsk', kv, Wv) * m
            energy = jnp.einsum('bhsk,bhtk->bhst', Q, K)
            S = energy.shape[-1]
            lengths = jnp.sum(energy[:, :, 0, :] != 0, axis=-1)
            cols = jnp.arange(S)
            energy = jnp.where(cols[None, None, None, :] >= lengths[:, :, None, None], -jnp.inf, energy)
            if causal:
                energy = jnp.where(cols[None, :] > cols[:, None], -jnp.inf, energy)
            dk = Wq.shape[-1]
            score = jax.nn.softmax(energy / jnp.sqrt(jnp.asarray(dk, energy.dtype)), axis=-1)
            out = jnp.einsum('bhst,bhtk->bhsk', score, V) * m
            B, H, Sx, dkk = out.shape
            return out.transpose(0, 2, 1, 3).reshape(B, Sx, H * dkk)
        mask0 = 1.0 - jnp.all(x == 0, axis=2, keepdims=True).astype(x.dtype)
        z = _mha(x, x, Wq1, Wk1, Wv1, mask0, causal=True)
        x1 = _layernorm(x + z, ln1_g, ln1_b)
        mask1 = 1.0 - jnp.all(x1 == 0, axis=2, keepdims=True).astype(x1.dtype)
        z = _mha(x1, context, Wq2, Wk2, Wv2, mask1, causal=False)
        x2 = _layernorm(x1 + z, ln2_g, ln2_b)
        z = jnp.maximum(x2 @ fc1_w.T + fc1_b, 0.0) * mask0
        z = (z @ fc2_w.T + fc2_b) * mask0
        return _layernorm(x2 + z, ln3_g, ln3_b)

    def _L1_xattn_ref(q_x, kv_x, Wq, Wkv, Wo, bo, ln_q_g, ln_q_b, ln_kv_g, ln_kv_b, W1, b1, W2, b2):
        import jax, jax.numpy as jnp
        import numpy as np
        D = 128
        H = 16
        HD = D // H
        DFF = 4 * D
        LN_EPS = 1e-05

        def layernorm(x, gamma, beta):
            mu = jnp.mean(x, axis=-1, keepdims=True)
            var = jnp.mean(jnp.square(x - mu), axis=-1, keepdims=True)
            return (x - mu) * jax.lax.rsqrt(var + LN_EPS) * gamma + beta
        B, Nq, _ = q_x.shape
        Nk = kv_x.shape[1]
        scale = HD ** (-0.5)
        q = layernorm(q_x, ln_q_g, ln_q_b) @ Wq.T
        kv = layernorm(kv_x, ln_kv_g, ln_kv_b) @ Wkv.T
        q = q.reshape(B, Nq, H, HD).transpose(0, 2, 1, 3)
        kv = kv.reshape(B, Nk, 2, H, HD).transpose(2, 0, 3, 1, 4)
        k, v = (kv[0], kv[1])
        attn = jnp.einsum('bhqd,bhkd->bhqk', q, k) * scale
        attn = jax.nn.softmax(attn, axis=-1)
        out = jnp.einsum('bhqk,bhkd->bhqd', attn, v)
        out = out.transpose(0, 2, 1, 3).reshape(B, Nq, D)
        x = q_x + out @ Wo.T + bo
        h = jax.nn.silu(x @ W1.T + b1)
        x = x + h @ W2.T + b2
        return x

    def _L2_xattn_ref(x, encoder_output, sa_wq, sa_wk, sa_wv, sa_wo, ca_wq, ca_wk, ca_wv, ca_wo, ffn_w1, ffn_b1, ffn_w2, ffn_b2, ln1_g, ln1_b, ln2_g, ln2_b, ln3_g, ln3_b):
        import jax, jax.numpy as jnp
        import numpy as np
        B, S, D, H, FF = (2, 256, 128, 16, 512)
        DK = D // H
        LN_EPS = 1e-05

        def layer_norm(x, g, b):
            mu = jnp.mean(x, axis=-1, keepdims=True)
            var = jnp.var(x, axis=-1, keepdims=True)
            return (x - mu) * jax.lax.rsqrt(var + LN_EPS) * g + b

        def split_heads(t):
            b, l, _ = t.shape
            return t.reshape(b, l, H, DK).transpose(0, 2, 1, 3)

        def mha(q_in, k_in, v_in, wq, wk, wv, wo, causal):
            q = split_heads(q_in @ wq)
            k = split_heads(k_in @ wk)
            v = split_heads(v_in @ wv)
            attn = jnp.einsum('bhqd,bhkd->bhqk', q, k) * DK ** (-0.5)
            if causal:
                lq = q.shape[2]
                mask = jnp.tril(jnp.ones((lq, lq), dtype=bool))
                attn = jnp.where(mask, attn, -jnp.inf)
            attn = jax.nn.softmax(attn, axis=-1)
            out = jnp.einsum('bhqk,bhkd->bhqd', attn, v)
            out = out.transpose(0, 2, 1, 3).reshape(q_in.shape[0], q_in.shape[1], D)
            return out @ wo
        h = layer_norm(x, ln1_g, ln1_b)
        x = x + mha(h, h, h, sa_wq, sa_wk, sa_wv, sa_wo, causal=True)
        h = layer_norm(x, ln2_g, ln2_b)
        x = x + mha(h, encoder_output, encoder_output, ca_wq, ca_wk, ca_wv, ca_wo, causal=False)
        h = layer_norm(x, ln3_g, ln3_b)
        x = x + (jax.nn.relu(h @ ffn_w1 + ffn_b1) @ ffn_w2 + ffn_b2)
        return x

    def _L3_xattn_ref(queries, keys, values, Wq, bq, Wk, bk, Wv, bv, gamma, beta, Wff, bff):
        import jax, jax.numpy as jnp
        import numpy as np
        NEG = -4294967295.0
        EPS = 1e-08
        H = 4
        L = 3

        def _layer_norm(x, g, b):
            mean = jnp.mean(x, axis=-1, keepdims=True)
            std = jnp.std(x, axis=-1, keepdims=True, ddof=1)
            return g * (x - mean) / (std + EPS) + b

        def _mha_layer(q, k, v, Wq, bq, Wk, bk, Wv, bv, gamma, beta):
            B, Sq, d = q.shape
            Sk = k.shape[1]
            dh = d // H
            Q = jax.nn.relu(q @ Wq + bq)
            K = jax.nn.relu(k @ Wk + bk)
            V = jax.nn.relu(v @ Wv + bv)
            Qh = Q.reshape(B, Sq, H, dh).transpose(2, 0, 1, 3)
            Kh = K.reshape(B, Sk, H, dh).transpose(2, 0, 1, 3)
            Vh = V.reshape(B, Sk, H, dh).transpose(2, 0, 1, 3)
            scores = jnp.einsum('hbqd,hbkd->hbqk', Qh, Kh) / jnp.sqrt(jnp.float32(dh))
            key_mask = jnp.sign(jnp.abs(jnp.sum(k, axis=-1)))
            scores = jnp.where(key_mask[None, :, None, :] == 0.0, NEG, scores)
            attn = jax.nn.softmax(scores, axis=-1)
            query_mask = jnp.sign(jnp.abs(jnp.sum(q, axis=-1)))
            attn = attn * query_mask[None, :, :, None]
            out = jnp.einsum('hbqk,hbkd->hbqd', attn, Vh)
            out = out.transpose(1, 2, 0, 3).reshape(B, Sq, d)
            out = out + q
            return _layer_norm(out, gamma, beta)
        q, k, v = (queries, keys, values)
        enc = q
        for i in range(L):
            enc = _mha_layer(q, k, v, Wq[i], bq[i], Wk[i], bk[i], Wv[i], bv[i], gamma[i], beta[i])
            enc = jax.nn.leaky_relu(enc @ Wff[i] + bff[i], negative_slope=0.2) + enc
            q, k, v = (enc, enc, enc)
        return enc
    x = _L0_xattn_ref(x, ctx_1024, L0_xattn_Wq1, L0_xattn_Wk1, L0_xattn_Wv1, L0_xattn_Wq2, L0_xattn_Wk2, L0_xattn_Wv2, L0_xattn_ln1_g, L0_xattn_ln1_b, L0_xattn_ln2_g, L0_xattn_ln2_b, L0_xattn_ln3_g, L0_xattn_ln3_b, L0_xattn_fc1_w, L0_xattn_fc1_b, L0_xattn_fc2_w, L0_xattn_fc2_b)
    x = _L1_xattn_ref(x, ctx_1024, L1_xattn_Wq, L1_xattn_Wkv, L1_xattn_Wo, L1_xattn_bo, L1_xattn_ln_q_g, L1_xattn_ln_q_b, L1_xattn_ln_kv_g, L1_xattn_ln_kv_b, L1_xattn_W1, L1_xattn_b1, L1_xattn_W2, L1_xattn_b2)
    x = _L2_xattn_ref(x, ctx_1024, L2_xattn_sa_wq, L2_xattn_sa_wk, L2_xattn_sa_wv, L2_xattn_sa_wo, L2_xattn_ca_wq, L2_xattn_ca_wk, L2_xattn_ca_wv, L2_xattn_ca_wo, L2_xattn_ffn_w1, L2_xattn_ffn_b1, L2_xattn_ffn_w2, L2_xattn_ffn_b2, L2_xattn_ln1_g, L2_xattn_ln1_b, L2_xattn_ln2_g, L2_xattn_ln2_b, L2_xattn_ln3_g, L2_xattn_ln3_b)
    x = _L3_xattn_ref(x, ctx_1024, ctx_1024, L3_xattn_Wq, L3_xattn_bq, L3_xattn_Wk, L3_xattn_bk, L3_xattn_Wv, L3_xattn_bv, L3_xattn_gamma, L3_xattn_beta, L3_xattn_Wff, L3_xattn_bff)
    return x

_drawn_inputs = setup_inputs


def setup_inputs(seed=0):
    import zlib

    import numpy as np

    out = dict(_drawn_inputs(seed))
    spreads = {'L0_xattn_ln1_g': (1.0, 0.2),
     'L0_xattn_ln1_b': (0.0, 0.1),
     'L0_xattn_ln2_g': (1.0, 0.2),
     'L0_xattn_ln2_b': (0.0, 0.1),
     'L0_xattn_ln3_g': (1.0, 0.2),
     'L0_xattn_ln3_b': (0.0, 0.1),
     'L0_xattn_fc1_b': (0.0, 0.624),
     'L0_xattn_fc2_b': (0.0, 0.1),
     'L1_xattn_bo': (0.0, 0.1),
     'L1_xattn_ln_q_g': (1.0, 0.6),
     'L1_xattn_ln_q_b': (0.0, 2.0),
     'L1_xattn_ln_kv_g': (1.0, 0.6),
     'L1_xattn_ln_kv_b': (0.0, 0.8),
     'L1_xattn_b1': (0.0, 0.275),
     'L1_xattn_b2': (0.0, 0.1),
     'L2_xattn_ffn_b1': (0.0, 0.1),
     'L2_xattn_ffn_b2': (0.0, 0.1),
     'L2_xattn_ln1_g': (1.0, 0.2),
     'L2_xattn_ln1_b': (0.0, 0.1),
     'L2_xattn_ln2_g': (1.0, 0.2),
     'L2_xattn_ln2_b': (0.0, 0.439),
     'L2_xattn_ln3_g': (1.0, 0.2),
     'L2_xattn_ln3_b': (0.0, 0.1),
     'L3_xattn_bq': (0.0, 0.8),
     'L3_xattn_bk': (0.0, 2.0),
     'L3_xattn_bv': (0.0, 0.1),
     'L3_xattn_gamma': (1.0, 0.2),
     'L3_xattn_beta': (0.0, 0.1),
     'L3_xattn_bff': (0.0, 0.1)}
    factors = {'L0_xattn_Wq1': 8.0,
     'L0_xattn_Wk1': 8.0,
     'L0_xattn_Wq2': 8.0,
     'L0_xattn_Wk2': 8.0,
     'L1_xattn_Wq': 28.836,
     'L3_xattn_Wq': 8.0,
     'L3_xattn_Wk': 8.0}
    for name, (base, spread) in spreads.items():
        noise = np.random.default_rng([zlib.crc32(name.encode()), seed]).standard_normal(out[name].shape)
        drawn = base * np.exp(spread * noise) if base else spread * noise
        out[name] = jnp.asarray(drawn.astype(out[name].dtype))
    for name, factor in factors.items():
        out[name] = (out[name] * factor).astype(out[name].dtype)
    return out
```

```python
from contextlib import ExitStack

import numpy as np

import concourse.bass as bass
from concourse import mybir

F32 = mybir.dt.float32
BF16 = mybir.dt.bfloat16
ACT = mybir.ActivationFunctionType
ALU = mybir.AluOpType
AX = mybir.AxisListType

P = 128
SEQS, S, D = 64, 64, 128
STREAMS = 2
NB = 8
NT = NB // 2
TOK = NB * S
GROUPS = SEQS // (STREAMS * NB)
BIG = 1.0e30
ABSENT = 4294967296.0 * 32.0 ** 0.5

ATTS = range(8)
PAIRS = [8, 8, 8, 8, 8, 2, 2, 2]
CAUSAL = [True, False, False, True, False, False, False, False]
KEYMASK = ["length", "length", None, None, None, "sum", "sum", "sum"]
QUERYMASK = [True, True, False, False, False, True, True, True]
KV_FROM = ["xf", "kf", "kf", "xf", "cf", "cf", "xf", "xf"]
BETWEEN = [
    ["ctx", "x"],
    ["x1", "kv"],
    ["x1", "fc1", "fc2", "q", "kv"],
    ["o", "wo", "x", "w1", "w2", "q"],
    ["o", "wo", "q"],
    ["o", "wo", "q", "w1", "w2", "x"],
    ["x1", "ff", "x"],
    ["x1", "ff", "x"],
    ["x1", "ff", "out"],
]


def steps_before(a):
    steps = list(BETWEEN[a])
    if a < len(ATTS):
        steps += ["pk", "pq", "pv"]
        if KEYMASK[a] == "length":
            steps += ["first", "length", "maskrow"]
        if KEYMASK[a] == "sum":
            steps += ["ksum", "maskrow"]
        steps += ["rowmax0", "rowmax1", "maxrow"]
    return steps


WEIGHTS = (["wq0", "wk0", "wv0", "wq1", "wk1", "wv1", "fc1", "fc2", "wq2", "wk2", "wv2", "wo2"]
           + [f"u2_{c}" for c in range(4)] + [f"d2_{c}" for c in range(4)]
           + ["wq3", "wk3", "wv3", "wo3", "wq4", "wk4", "wv4", "wo4"]
           + [f"u4_{c}" for c in range(4)] + [f"d4_{c}" for c in range(4)]
           + [f"{w}{a}" for a in (5, 6, 7) for w in ("wq", "wk", "wv", "ff")])
COLUMNS = (["fc1_b", "q2_g", "q2_b", "kv2_g", "kv2_b"] + [f"u2_b{c}" for c in range(4)]
           + ["q3_g", "q3_b", "q4_g", "q4_b", "q5_g", "q5_b"] + [f"u4_b{c}" for c in range(4)]
           + ["bq5", "bq6", "bq7", "bk5", "bk6", "bk7"])
ROWS = ["n1_g", "n1_b", "n2_g", "n2_b", "n3_g", "n3_b", "fc2_b", "bo2", "d2_b", "d4_b",
        "e6_g", "e7_g", "e8_g", "e6_b", "e7_b", "e8_b", "bv5", "bv6", "bv7", "bff6", "bff7", "bff8"]
CONST32 = [("ident", 128), ("pair8", 8), ("pair2", 2), ("par8", 2), ("par2", 2), ("pos", 1), ("ones", 128),
           ("own8", 8), ("own2", 16)]
CONST16 = [("identb", 128), ("fold", 64), ("sel8", 1024), ("sel2", 128), ("samepar", 128),
           ("causB", 64), ("causA", 64)]


def constants():
    p = np.arange(P)
    eye = np.eye(P)
    c = {"ident": eye, "identb": eye, "ones": np.ones((P, 128)), "pos": (p % S)[:, None]}
    for n, pairs in (("8", 8), ("2", 2)):
        dh = D // (2 * pairs)
        c["pair" + n] = (p // (2 * dh))[:, None] == np.arange(pairs)
        c["par" + n] = (p // dh % 2)[:, None] == np.arange(2)
    c["fold"] = (p % S)[:, None] == np.arange(S)
    parity = np.arange(P) // S
    c["own8"] = (p % 8)[:, None] == np.arange(8)
    c["sel8"] = ((p // 16)[:, None, None] == np.arange(8)[None, :, None]) & \
        ((p // 8 % 2)[:, None, None] == parity[None, None, :])
    r = p % 32
    c["own2"] = ((r // 4)[:, None, None] == np.arange(8)[None, :, None]) & ((r % 2)[:, None, None] == np.arange(2))
    c["sel2"] = (r // 2 % 2)[:, None] == parity[None, :]
    c["samepar"] = parity[:, None] == parity[None, :]
    c["causB"] = -BIG * ((p % S)[:, None] > np.arange(S)[None, :])
    c["causA"] = -BIG * (np.arange(S)[None, :] > (p % S)[:, None])
    flat = lambda names: np.concatenate([np.reshape(c[n], (P, w)).astype(np.float32) for n, w in names], 1)
    return flat(CONST32), flat(CONST16)


class Signal:

    def __init__(self, ctx, nc, name, known):
        self.sem = ctx.enter_context(nc.semaphore(name))
        self.name, self.known, self.count = name, known, 0
        self.events = {}

    def mark(self, *event, by=1):
        self.count += by
        self.events[event] = self.count
        return self.sem, by

    def at(self, *event):
        return self.sem, (self.known[self.name][event] if self.known else 1)


class Banks:

    def __init__(self, ctx, nc, known):
        self.filled = [ctx.enter_context(nc.semaphore(f"filled{k}")) for k in range(8)]
        self.tensor = [ctx.enter_context(nc.psum_tensor(f"bank{k}", [P, 512], F32)) for k in range(8)]
        self.known = known
        self.uses, self.readers, self.last, self.turn, self.place = [0] * 8, {}, {}, {}, {}

    def take(self, pe, ring, *use):
        n = self.turn[ring] = self.turn.get(ring, -1) + 1
        k = ring[n % len(ring)]
        if self.known and k in self.last:
            for sem, count in self.known["readers"][self.last[k]].items():
                pe.wait_ge(self.sems[sem], count)
        self.last[k] = use
        self.uses[k] += 1
        self.place[use] = (k, self.uses[k])
        return self.tensor[k]

    def full(self, *use):
        return self.filled[self.place[use][0]], 1

    def of(self, *use):
        return self.tensor[self.known["place"][use][0] if self.known else 0]

    def ready(self, *use):
        if not self.known:
            return self.filled[0], 1
        k, n = self.known["place"][use]
        return self.filled[k], n

    def drain(self, use, signal, *event):
        sem, by = signal.mark(*event)
        self.readers.setdefault(use, {})[signal.name] = signal.count
        return sem, by


NPT = 4
RING_S = (0, 1, 2, 3)
RING_O = (4, 5)
RING_M = (6, 7)


def network(nc, x, ctx_in, weights, columns, rows, const32, const16, out, known):
    x_g = x.rearrange("(i s j p) t d -> i s (p t) j d", i=GROUPS, s=STREAMS, p=2)
    c_g = ctx_in.rearrange("(i s j p) t d -> i s (p t) j d", i=GROUPS, s=STREAMS, p=2)
    o_g = out.rearrange("(i s j p) t d -> i s (p t) j d", i=GROUPS, s=STREAMS, p=2)

    with ExitStack() as ctx:
        def sb(name, shape, dt=F32):
            return ctx.enter_context(nc.sbuf_tensor(name, shape, dt))

        def per_stream(name, shape, dt=F32):
            return [sb(f"{name}{s}", shape, dt) for s in range(STREAMS)]

        W_all = sb("W_all", [P, len(WEIGHTS), 128])
        cols = sb("cols", [P, len(COLUMNS)])
        half = sb("half", [P, 4])
        row = sb("row", [P, len(ROWS), 128])
        c32 = sb("c32", [P, sum(w for _, w in CONST32)])
        c16 = sb("c16", [P, sum(w for _, w in CONST16)], BF16)

        def pick(buf, names, name):
            at = 0
            for n, w in names:
                if n == name:
                    return buf[:, at:at + w]
                at += w
            raise KeyError(name)

        def W(name):
            return W_all[:, WEIGHTS.index(name), :]

        def col(name):
            i = COLUMNS.index(name)
            return cols[:, i:i + 1]

        def rowb(name):
            return row[:, ROWS.index(name), :]

        def K32(name):
            return pick(c32, CONST32, name)

        def K16(name):
            return pick(c16, CONST16, name)

        X = per_stream("X", [P, NT, 128])
        C = per_stream("C", [P, NT, 128])
        Y = per_stream("Y", [P, NT, 128])
        Y2 = per_stream("Y2", [P, NT, 128])
        O = per_stream("O", [P, NT, 128])
        xf = per_stream("xf", [P, TOK])
        kf = per_stream("kf", [P, TOK])
        cf = per_stream("cf", [P, TOK])
        of = kf
        hid = per_stream("hid", [P, 4, TOK])
        tnh = per_stream("tnh", [P, 2, TOK])
        qs = per_stream("qs", [P, TOK])
        ks = per_stream("ks", [P, TOK])
        qb = per_stream("qb", [P, TOK], BF16)
        kb = per_stream("kb", [P, TOK], BF16)
        Qpar = per_stream("Qpar", [P, NB, 2, S], BF16)
        Kpar = per_stream("Kpar", [P, NB, 2, S])
        Qpair = per_stream("Qpair", [P, NB * 8 * S])
        Kpair = per_stream("Kpair", [P, NB * 8 * S], BF16)
        V8 = per_stream("V8", [P, NB, 8, 2, 9])
        V2 = per_stream("V2", [P, NB, 2, 2, 33])
        mx = per_stream("mx", [P, NB * 8])
        nm8 = per_stream("nm8", [P, NB, 2, 8], BF16)
        nm2 = per_stream("nm2", [P, NB, 2, 2], BF16)
        lm8 = per_stream("lm8", [P, NB, 2, 8], BF16)
        lm2 = per_stream("lm2", [P, NB, 2, 2], BF16)
        mrow = per_stream("mrow", [P, 1024], BF16)
        lrow = per_stream("lrow", [P, 1024], BF16)
        nz = per_stream("nz", [P, NB * 8], BF16)
        km = per_stream("km", [P, NB * 8], BF16)
        km1 = per_stream("km1", [P, NB])
        rd = per_stream("rd", [P, 2, 16])
        rq = per_stream("rq", [P, 2, 16])
        stats = per_stream("stats", [P, NT, 6])
        mv = per_stream("mv", [P, NT, 2])
        rstd = per_stream("rstd", [P, NT])
        ve = per_stream("ve", [P, NT])
        dev = per_stream("dev", [P, NT])
        am = per_stream("am", [P, NT])
        m0 = per_stream("m0", [P, NT])
        qm = per_stream("qm", [P, NT])
        PT = sb("PT", [P, NPT, 512])
        expo = sb("expo", [P, 3, NT])

        banks = Banks(ctx, nc, known and known["banks"])
        signals = {}

        def sig(name):
            if name not in signals:
                signals[name] = Signal(ctx, nc, name, known and known["signals"])
            return signals[name]

        setup = ctx.enter_context(nc.semaphore("setup"))
        setdve = ctx.enter_context(nc.semaphore("setdve"))
        loaded_w = ctx.enter_context(nc.semaphore("loaded_w"))

        x_in = [sig(f"x_in{s}") for s in range(STREAMS)]
        c_in = [sig(f"c_in{s}") for s in range(STREAMS)]
        x_out = [sig(f"x_out{s}") for s in range(STREAMS)]
        operand = sig("operand")
        probs = sig("probs")
        vec = sig("vec")
        pool = sig("pool")
        banks.sems = {n: signals[n].sem for n in signals}

        with nc.Block() as block:
            @block.sync
            def _(sp):
                sp.dma_start(c32[:], const32).then_inc(loaded_w, 16)
                sp.dma_start(c16[:], const16).then_inc(loaded_w, 16)
                sp.dma_start(cols[:], columns).then_inc(loaded_w, 16)
                sp.dma_start(W_all[:], weights.rearrange("p (n c) -> p n c", c=128)).then_inc(loaded_w, 16)
                sp.dma_start(row[:], rows.broadcast_to((P, len(ROWS), 128))).then_inc(loaded_w, 16)
                sp.wait_ge(loaded_w, 80)

            @block.gpsimd
            def _(g):
                n = 0
                for s in range(STREAMS):
                    for buf in (nm8, nm2, lm8, lm2, V8, V2):
                        g.memset(buf[s][:], 0.0).then_inc(setup, 1)
                        n += 1
                g.memset(expo[:, 0, :], -0.5).then_inc(setup, 1)
                g.memset(expo[:, 1, :], 0.5).then_inc(setup, 1)
                g.memset(expo[:, 2, :], -1.0).then_inc(setup, 1)
                g.wait_ge(setup, n + 3)
                for s in range(STREAMS):
                    for par in range(2):
                        rows_ = slice(64 * par, 64 * par + 64)
                        g.memset(V8[s][rows_, :, :, par, 8:9], 1.0).then_inc(setup, 1)
                        g.memset(V2[s][rows_, :, :, par, 32:33], 1.0).then_inc(setup, 1)
                g.wait_ge(setup, n + 3 + 8)

            @block.vector
            def _(v):
                v.wait_ge(loaded_w, 80)
                i = COLUMNS.index("u2_b0")
                v.tensor_scalar(half[:], cols[:, i:i + 4], 0.5, None, ALU.mult).then_inc(setdve, 1)
                v.wait_ge(setdve, 1)
        nc.all_engine_barrier()

        def unit(a):
            n = PAIRS[a] * S
            return NB * n // 512, 512 // n, n

        def tiles(ap):
            return ap.rearrange("p (j c) -> p j c", j=NT)

        def half_units(name, units):
            return range(units // 2) if name == "rowmax0" else range(units // 2, units)

        def exp_number(a, s, u):
            return sum(STREAMS * unit(i)[0] for i in range(a)) + s * unit(a)[0] + u

        def last_pair(a, u):
            return (unit(a)[1] * (u + 1) - 1) // 2

        kv_of = lambda a, s: {"xf": xf, "kf": kf, "cf": cf}[KV_FROM[a]][s]

        def kv_event(a, s):
            if KV_FROM[a] == "cf":
                return "ctx", 0, s
            if KV_FROM[a] == "kf":
                return "kv", a, s
            return q_step(a), a, s

        def q_step(a):
            return {0: "x", 1: "x1", 2: "q", 3: "q", 4: "q", 5: "x", 6: "x", 7: "x"}[a]

        def walk(loop_unit, step):
            for s in range(STREAMS):
                for name in steps_before(0):
                    step(name, 0, s)
            for a in ATTS:
                for s in range(STREAMS):
                    other, before = (1 - s, a) if s == 0 else (1 - s, a + 1)
                    todo = [] if (s == 0 and a == 0) else steps_before(before)
                    units = unit(a)[0]
                    for u in range(units + 1):
                        loop_unit(a, s, u)
                        for name in todo[u * len(todo) // (units + 1):(u + 1) * len(todo) // (units + 1)]:
                            step(name, before, other)
            for name in steps_before(len(ATTS)):
                step(name, len(ATTS), 1)

        with nc.Fori(0, GROUPS) as g:
            with nc.Block() as block:
                @block.sync
                def _(sp):
                    for s in range(STREAMS):
                        sp.dma_start(C[s][:], c_g[g, s]).then_inc(*c_in[s].mark(by=16))
                        sp.dma_start(X[s][:], x_g[g, s]).then_inc(*x_in[s].mark(by=16))
                    for s in range(STREAMS):
                        sp.wait_ge(*pool.at("enc", 8, s))
                        sp.dma_start(o_g[g, s], X[s][:]).then_inc(*x_out[s].mark(by=16))
                    for s in range(STREAMS):
                        sp.wait_ge(*x_out[s].at())

                @block.tensor
                def _(pe):
                    def turn(src, use):
                        t = banks.take(pe, RING_M, *use)
                        for j in range(NT):
                            mm = pe.transpose(t[:, 128 * j:128 * j + 128], src[:, j, :], K32("ident"))
                        mm.then_inc(*banks.full(*use))

                    def token_major(src, name, use):
                        t = banks.take(pe, RING_M, *use)
                        for j in range(NT):
                            mm = pe.matmul(t[:, 128 * j:128 * j + 128], src[:, 128 * j:128 * j + 128], W(name),
                                           start=True, stop=True)
                        mm.then_inc(*banks.full(*use))

                    def feature_major(src, name, use):
                        t = banks.take(pe, RING_M, *use)
                        pe.matmul(t[:], W(name), src[:], start=True, stop=True).then_inc(*banks.full(*use))

                    def step(name, a, s):
                        use = (name, a, s)
                        if name == "ctx":
                            pe.wait_ge(*c_in[s].at())
                            turn(C[s], use)
                        elif name == "x":
                            if a == 0:
                                pe.wait_ge(*x_in[s].at())
                            elif a in (3, 5):
                                pe.wait_ge(*vec.at("wo" if a == 3 else "w2", a, s))
                            else:
                                pe.wait_ge(*pool.at("enc", a, s))
                            turn(X[s], use)
                        elif name == "x1":
                            pe.wait_ge(*vec.at("x1", a, s))
                            turn(X[s], use)
                        elif name == "q":
                            pe.wait_ge(*vec.at("q", a, s))
                            turn(Y[s], use)
                        elif name == "kv":
                            pe.wait_ge(*vec.at("kv", a, s))
                            turn(Y2[s], use)
                        elif name == "fc1":
                            pe.wait_ge(*operand.at("x1", a, s))
                            feature_major(xf[s], "fc1", use)
                        elif name == "fc2":
                            pe.wait_ge(*operand.at("fc1", a, s))
                            token_major(hid[s][:, 0, :], "fc2", use)
                        elif name == "o":
                            pe.wait_ge(*vec.at("O", a - 1, s, NT - 1))
                            turn(O[s], use)
                        elif name == "wo":
                            pe.wait_ge(*operand.at("o", a, s))
                            token_major(of[s], f"wo{a - 1}", use)
                        elif name == "w1":
                            pe.wait_ge(*operand.at("x" if a == 3 else "q", a, s))
                            for c in range(4):
                                feature_major(xf[s], f"u{a - 1}_{c}", (name, a, s, c))
                        elif name == "w2":
                            if a == 3:
                                pe.wait_ge(*vec.at("hid", a, s, 3))
                            else:
                                pe.wait_ge(*operand.at("hid", a, s, 3))
                            t = banks.take(pe, RING_M, *use)
                            for j in range(NT):
                                for c in range(4):
                                    mm = pe.matmul(t[:, 128 * j:128 * j + 128], hid[s][:, c, 128 * j:128 * j + 128],
                                                   W(f"d{a - 1}_{c}"), start=c == 0, stop=c == 3)
                            mm.then_inc(*banks.full(*use))
                        elif name == "ff":
                            pe.wait_ge(*operand.at("x1", a, s))
                            t = banks.take(pe, RING_M, *use)
                            for j in range(NT):
                                out_j = t[:, 128 * j:128 * j + 128]
                                pe.matmul(out_j, xf[s][:, 128 * j:128 * j + 128], W(f"ff{a - 1}"),
                                          start=True, stop=False)
                                mm = pe.matmul(out_j, K32("ones")[0:1, :], rowb(f"bff{a}")[0:1, :],
                                               start=False, stop=True)
                            mm.then_inc(*banks.full(*use))
                        elif name == "pk":
                            pe.wait_ge(*operand.at(*kv_event(a, s)))
                            feature_major(kv_of(a, s), f"wk{a}", use)
                        elif name == "pq":
                            pe.wait_ge(*operand.at(q_step(a), a, s))
                            feature_major(xf[s], f"wq{a}", use)
                        elif name == "pv":
                            src, pairs = kv_of(a, s), PAIRS[a]
                            t = banks.take(pe, RING_M, *use)
                            w = W(f"wv{a}").rearrange("p (h r d) -> p h r d", h=pairs, r=2)
                            for b in range(NB):
                                for par in range(2):
                                    out_b = t[64 * par:64 * par + 64, S * b:S * b + S]
                                    mm = pe.matmul(out_b, src[:, S * b:S * b + S], w[:, :, par, :],
                                                   start=True, stop=pairs == 8)
                                    if pairs == 2:
                                        bias = rowb(f"bv{a}")[0:1, :].rearrange("p (h r d) -> p h r d", h=2, r=2)
                                        mm = pe.matmul(out_b, K32("ones")[0:1, 0:64], bias[:, :, par, :],
                                                       start=False, stop=True)
                            mm.then_inc(*banks.full(*use))
                        elif name == "first":
                            pe.wait_ge(*vec.at("Qpair", a, s))
                            t = banks.take(pe, RING_M, *use)
                            q = Qpair[s].rearrange("p (b h q) -> p b h q", b=NB, q=S)
                            for b in range(NB):
                                mm = pe.matmul(t[:, 8 * b:8 * b + 8], Kpar[s][:, b].rearrange("p r t -> p (r t)"), q[:, b, :, 0],
                                               start=True, stop=True)
                            mm.then_inc(*banks.full(*use))
                        elif name == "length":
                            pe.wait_ge(*vec.at("nz", a, s))
                            t = banks.take(pe, RING_M, *use)
                            pe.matmul(t[:, 0:64], K16("samepar"), nz[s][:], start=True, stop=True
                                      ).then_inc(*banks.full(*use))
                        elif name == "ksum":
                            t = banks.take(pe, RING_M, *use)
                            src = kv_of(a, s)
                            for b in range(NB):
                                for r in (0, 64):
                                    mm = pe.matmul(t[r:r + 64, b:b + 1], src[:, S * b:S * b + S], K32("ones")[:, 0:1],
                                                   start=True, stop=True)
                            mm.then_inc(*banks.full(*use))
                        elif name in ("maskrow", "maxrow"):
                            pe.wait_ge(*vec.at("lm" if name == "maskrow" else "nm", a, s))
                            t = banks.take(pe, RING_M, *use)
                            m = {("maskrow", 8): lm8, ("maskrow", 2): lm2, ("maxrow", 8): nm8, ("maxrow", 2): nm2}[
                                name, PAIRS[a]][s]
                            n = NB * 2 * PAIRS[a]
                            pe.matmul(t[0:n, 0:S], m.rearrange("p b r h -> p (b r h)"), K16("fold"),
                                      start=True, stop=True).then_inc(*banks.full(*use))
                        elif name in ("rowmax0", "rowmax1"):
                            units = unit(a)[0]
                            pe.wait_ge(*vec.at("Qpar", a, s))
                            if KEYMASK[a]:
                                pe.wait_ge(*vec.at("lrow", a, s))
                            for u in half_units(name, units):
                                scores("A", a, s, u, Qpar[s], Kpair[s])

                    def mask_terms(kind, a, s, u):
                        seqs, pairs = unit(a)[1], PAIRS[a]
                        terms = []
                        if CAUSAL[a]:
                            terms.append((K16("identb"), K16("caus" + kind).unsqueeze(1).broadcast_to((P, 8, S))))
                        if kind == "B" and KEYMASK[a]:
                            m = km[s][:, 8 * u:8 * u + 8]
                            terms.append((K16("identb"), m.unsqueeze(2).broadcast_to((P, 8, S))))
                        spread = [lrow] if kind == "A" and KEYMASK[a] else [mrow] if kind == "B" else []
                        for r in spread:
                            if pairs == 8:
                                sel = K16("sel8").rearrange("p (b c) -> p b c", b=NB)[:, u, :]
                                terms.append((sel, r[s][:, 0:512]))
                            else:
                                terms.append((K16("sel2")[0:32, :], r[s][0:32, 512 * u:512 * u + 512]))
                        return terms

                    def scores(kind, a, s, u, stationary, moving):
                        units, seqs, n = unit(a)
                        t = banks.take(pe, RING_S, kind, a, s, u)
                        terms = mask_terms(kind, a, s, u)
                        m = moving[:, 0:NB * n].rearrange("p (b c) -> p b c", b=NB)
                        for i in range(seqs):
                            b = seqs * u + i
                            mm = pe.matmul(t[:, n * i:n * i + n], stationary[:, b].rearrange("p r t -> p (r t)"),
                                           m[:, b, :], start=i == 0,
                                           stop=i == seqs - 1 and not terms, skip_group_check=True)
                        for i, (fixed, spread) in enumerate(terms):
                            mm = pe.matmul(t[:], fixed, spread, start=False, stop=i == len(terms) - 1,
                                           skip_group_check=True)
                        mm.then_inc(*banks.full(kind, a, s, u))

                    def values(a, s, u):
                        units, seqs, n = unit(a)
                        pairs = PAIRS[a]
                        w = 2 * (D // (2 * pairs) + 1)
                        V = (V8 if pairs == 8 else V2)[s]
                        pe.wait_ge(*probs.at(a, s, u))
                        if u == 0:
                            pe.wait_ge(*operand.at("V", a, s))
                        p = PT[:, exp_number(a, s, u) % NPT, :].rearrange("p (b h q) -> p b h q", h=pairs, q=S)
                        for i in range(seqs):
                            b = seqs * u + i
                            if b % 2 == 0:
                                tile_o[0] = banks.take(pe, RING_O, "O", a, s, b // 2)
                            t = tile_o[0]
                            for h in range(pairs):
                                mm = pe.matmul(t[64 * (b % 2):64 * (b % 2) + 64, w * h:w * h + w], p[:, i, h, :],
                                               V[:, b, h].rearrange("p r d -> p (r d)"), start=True, stop=True)
                            if b % 2 == 1:
                                mm.then_inc(*banks.full("O", a, s, b // 2))

                    tile_o = [None]

                    def loop_unit(a, s, u):
                        if u < unit(a)[0]:
                            if u == 0:
                                pe.wait_ge(*vec.at("Qpair", a, s))
                                pe.wait_ge(*vec.at("mrow", a, s))
                            scores("B", a, s, u, Kpar[s], Qpair[s])
                        if u >= 1:
                            values(a, s, u - 1)

                    walk(loop_unit, step)

                @block.scalar
                def _(act):
                    def move(dst, src, use, *event, f=ACT.Copy, **kw):
                        act.wait_ge(*banks.ready(*use))
                        act.activation(dst, src, f, **kw).then_inc(*banks.drain(use, operand, *event))

                    def step(name, a, s):
                        use = (name, a, s)
                        full = banks.of(*use)[:] if name not in ("w1", "pv", "rowmax0", "rowmax1", "out") else None
                        if name == "ctx":
                            move(cf[s][:], full, use, *use)
                        elif name in ("x", "x1"):
                            move(xf[s][:], full, use, *use)
                        elif name == "q":
                            move(xf[s][:], full, use, *use, f=ACT.Identity, scale=col(f"q{a}_g"), bias=col(f"q{a}_b"))
                        elif name == "kv" and a == 1:
                            move(kf[s][:], full, use, *use)
                        elif name == "kv":
                            move(kf[s][:], full, use, *use, f=ACT.Identity, scale=col("kv2_g"), bias=col("kv2_b"))
                        elif name == "fc1":
                            move(hid[s][:, 0, :], full, use, *use, f=ACT.Relu, bias=col("fc1_b"))
                        elif name == "o":
                            move(of[s][:], full, use, *use)
                        elif name == "w1":
                            for c in range(4):
                                t = banks.of("w1", a, s, c)
                                if a == 3:
                                    if c >= 2:
                                        act.wait_ge(*vec.at("part", a, s, c - 2))
                                    move(tnh[s][:, c % 2, :], t[:], ("w1", a, s, c), "tanh", a, s, c, f=ACT.Tanh,
                                         scale=0.5, bias=half[:, c:c + 1])
                                else:
                                    move(hid[s][:, c, :], t[:], ("w1", a, s, c), "hid", a, s, c, f=ACT.Relu,
                                         bias=col(f"u4_b{c}"))
                        elif name == "ff":
                            move(Y[s].rearrange("p j c -> p (j c)"), full, use, "fifth", a, s, scale=0.2)
                        elif name in ("pk", "pq"):
                            plain, half_ = (ks, kb) if name == "pk" else (qs, qb)
                            kw = {}
                            if PAIRS[a] == 2:
                                kw = {"f": ACT.Relu, "bias": col(f"b{name[1]}{a}")}
                            move(half_[s][:], full, use, name + "b", a, s, **kw)
                            move(plain[s][:], full, use, name, a, s, **kw)
                        elif name == "pv":
                            pairs = PAIRS[a]
                            dh = D // (2 * pairs)
                            V = (V8 if pairs == 8 else V2)[s]
                            t = banks.of(*use)[:].rearrange("p (b h d) -> p b h d", b=NB, h=pairs)
                            for par in range(2):
                                r = slice(64 * par, 64 * par + 64)
                                move(V[r, :, :, par, 0:dh], t[r], use, *(("V", a, s) if par else ("V0", a, s)),
                                     f=ACT.Relu if pairs == 2 else ACT.Copy)

                    def loop_unit(a, s, u):
                        if u == unit(a)[0]:
                            return
                        n = exp_number(a, s, u)
                        if n >= NPT:
                            act.wait_ge(*banks.ready("O", *exp_user[n - NPT]))
                        act.wait_ge(*banks.ready("B", a, s, u))
                        act.activation(PT[:, n % NPT, :], banks.of("B", a, s, u)[:], ACT.Exp,
                                       scale=float((D // (2 * PAIRS[a])) ** -0.5)
                                       ).then_inc(*banks.drain(("B", a, s, u), probs, a, s, u))

                    exp_user = {exp_number(a, s, u): (a, s, last_pair(a, u))
                                for a in ATTS for s in range(STREAMS) for u in range(unit(a)[0])}
                    walk(loop_unit, step)

                @block.vector
                def _(dve):
                    def moments(src, *tag):
                        for j in range(NT):
                            dve.bn_stats(stats[tag[-1]][:, j, :], src[:, j, :]).then_inc(*vec.mark("stats", *tag))
                        dve.wait_ge(*vec.at("stats", *tag))
                        for j in range(NT):
                            dve.bn_aggr(mv[tag[-1]][:, j, :], stats[tag[-1]][:, j, :]).then_inc(*vec.mark("mv", *tag))
                        dve.wait_ge(*pool.at("rstd", *tag))

                    def norm(dst, src, *tag):
                        s = tag[-1]
                        moments(src, *tag)
                        for j in range(NT):
                            dve.tensor_scalar(dst[:, j, :], src[:, j, :], mv[s][:, j, 0:1], rstd[s][:, j:j + 1],
                                              ALU.subtract, ALU.mult).then_inc(*vec.mark(*tag))

                    def norm_affine(name, *tag):
                        s = tag[-1]
                        moments(X[s], *tag)
                        for j in range(NT):
                            dve.scalar_tensor_tensor(out=Y[s][:, j, :], in0=X[s][:, j, :], scalar=mv[s][:, j, 0:1],
                                                     in1=rowb(name + "_g"), op0=ALU.subtract, op1=ALU.mult
                                                     ).then_inc(*vec.mark("scaled", *tag))
                        dve.wait_ge(*vec.at("scaled", *tag))
                        for j in range(NT):
                            dve.scalar_tensor_tensor(out=X[s][:, j, :], in0=Y[s][:, j, :], scalar=rstd[s][:, j:j + 1],
                                                     in1=rowb(name + "_b"), op0=ALU.mult, op1=ALU.add
                                                     ).then_inc(*vec.mark(*tag))

                    def present(a, s, op, absolute):
                        dve.tensor_reduce(am[s][:], X[s][:], AX.X, op, apply_absolute_value=absolute
                                          ).then_inc(*vec.mark("am", a, s))
                        dve.wait_ge(*vec.at("am", a, s))
                        dve.tensor_scalar(qm[s][:], am[s][:], 0.0, None, ALU.not_equal).then_inc(*vec.mark("qm", a, s))

                    def step(name, a, s):
                        use = (name, a, s)
                        r = [slice(0, 64), slice(64, 128)]
                        if name == "x":
                            if a == 0:
                                dve.wait_ge(*x_in[s].at())
                                present(a, s, ALU.max, True)
                                dve.wait_ge(*vec.at("qm", a, s))
                                dve.tensor_copy(m0[s][:], qm[s][:]).then_inc(*vec.mark("m0", s))
                            elif a >= 5:
                                dve.wait_ge(*(vec.at("w2", 5, s) if a == 5 else pool.at("enc", a, s)))
                                present(a, s, ALU.add, False)
                        elif name == "x1":
                            dve.wait_ge(*vec.at("O", a - 1, s, NT - 1))
                            dve.tensor_tensor(X[s][:], X[s][:], O[s][:], ALU.add).then_inc(*vec.mark("sum", a, s))
                            dve.wait_ge(*vec.at("sum", a, s))
                            norm_affine(f"n{a}" if a < 3 else f"e{a}", "x1", a, s)
                            if a == 1:
                                dve.wait_ge(*vec.at("x1", a, s))
                                present(a, s, ALU.max, True)
                        elif name == "kv" and a == 1:
                            dve.wait_ge(*c_in[s].at())
                            dve.wait_ge(*vec.at("qm", a, s))
                            for j in range(NT):
                                dve.tensor_scalar(Y2[s][:, j, :], C[s][:, j, :], qm[s][:, j:j + 1], None, ALU.mult
                                                  ).then_inc(*vec.mark(*use))
                        elif name == "kv":
                            dve.wait_ge(*banks.ready("kv", 1, s))
                            norm(Y2[s], C[s], *use)
                        elif name == "q":
                            if a > 2:
                                dve.wait_ge(*vec.at("w2" if a == 3 else "wo", a, s))
                            else:
                                dve.wait_ge(*vec.at("n3", a, s))
                            norm(Y[s], X[s], *use)
                        elif name == "fc2":
                            dve.wait_ge(*banks.ready(*use))
                            dve.tensor_tensor(Y[s][:], tiles(banks.of(*use)[:]),
                                              rowb("fc2_b").unsqueeze(1).broadcast_to((P, NT, 128)), ALU.add
                                              ).then_inc(*banks.drain(use, vec, "z", a, s))
                            dve.wait_ge(*vec.at("z", a, s))
                            for j in range(NT):
                                dve.scalar_tensor_tensor(out=X[s][:, j, :], in0=Y[s][:, j, :], scalar=m0[s][:, j:j + 1],
                                                         in1=X[s][:, j, :], op0=ALU.mult, op1=ALU.add
                                                         ).then_inc(*vec.mark("x2", a, s))
                            dve.wait_ge(*vec.at("x2", a, s))
                            norm_affine("n3", "n3", a, s)
                        elif name in ("wo", "w2"):
                            if a == 3 or name == "w2":
                                dve.wait_ge(*pool.at("bias", name, a, s))
                            dve.wait_ge(*banks.ready(*use))
                            dve.scalar_tensor_tensor(out=X[s].rearrange("p j c -> p (j c)"), in0=banks.of(*use)[:],
                                                     scalar=0.5 if use[:2] == ("w2", 3) else 1.0,
                                                     in1=X[s].rearrange("p j c -> p (j c)"), op0=ALU.mult, op1=ALU.add
                                                     ).then_inc(*banks.drain(use, vec, *use))
                        elif name == "ff":
                            dve.wait_ge(*operand.at("fifth", a, s))
                            y = Y[s].rearrange("p j c -> p (j c)")
                            dve.scalar_tensor_tensor(out=y, in0=banks.of(*use)[:], scalar=1.0, in1=y, op0=ALU.mult,
                                                     op1=ALU.max).then_inc(*banks.drain(use, vec, "leaky", a, s))
                        elif name == "w1" and a == 3:
                            for c in range(4):
                                t = banks.of("w1", a, s, c)
                                dve.wait_ge(*operand.at("tanh", a, s, c))
                                dve.scalar_tensor_tensor(out=hid[s][:, c, :], in0=t[:], scalar=col(f"u2_b{c}"),
                                                         in1=tnh[s][:, c % 2, :], op0=ALU.add, op1=ALU.mult
                                                         ).then_inc(*vec.mark("part", a, s, c))
                                dve.wait_ge(*vec.at("part", a, s, c))
                                dve.scalar_tensor_tensor(out=hid[s][:, c, :], in0=t[:], scalar=col(f"u2_b{c}"),
                                                         in1=hid[s][:, c, :], op0=ALU.add, op1=ALU.add
                                                         ).then_inc(*banks.drain(("w1", a, s, c), vec, "hid", a, s, c))
                        elif name in ("pk", "pq"):
                            kind = str(PAIRS[a])
                            pairs = PAIRS[a]
                            src16, src32 = (kb, ks) if name == "pk" else (qb, qs)
                            pair_src, par_src = (src16, src32) if name == "pk" else (src32, src16)
                            pair_dst, par_dst = (Kpair, Kpar) if name == "pk" else (Qpair, Qpar)
                            d = pair_dst[s][:, 0:NB * pairs * S].rearrange("p (b h t) -> p b h t", b=NB, h=pairs)
                            dve.wait_ge(*operand.at(name, a, s))
                            for h in range(pairs):
                                dve.tensor_scalar(d[:, :, h, :], pair_src[s].rearrange("p (b t) -> p b t", b=NB),
                                                  K32("pair" + kind)[:, h:h + 1], None, ALU.mult
                                                  ).then_inc(*vec.mark("Kpair" if name == "pk" else "Qpair", a, s))
                            for h in range(2):
                                dve.tensor_scalar(par_dst[s][:, :, h, :], par_src[s].rearrange("p (b t) -> p b t", b=NB),
                                                  K32("par" + kind)[:, h:h + 1], None, ALU.mult
                                                  ).then_inc(*vec.mark("Kpar" if name == "pk" else "Qpar", a, s))
                        elif name == "first":
                            dve.wait_ge(*banks.ready(*use))
                            dve.tensor_scalar(nz[s][:], banks.of(*use)[:, 0:64], 0.0, None, ALU.not_equal
                                              ).then_inc(*banks.drain(use, vec, "nz", a, s))
                        elif name == "length":
                            dve.wait_ge(*banks.ready(*use))
                            dve.tensor_scalar(km[s][:], banks.of(*use)[:, 0:64], K32("pos"), -BIG, ALU.is_le, ALU.mult
                                              ).then_inc(*banks.drain(use, vec, "km", a, s))
                            dve.wait_ge(*vec.at("km", a, s))
                            for h in range(2):
                                dve.tensor_copy(lm8[s][r[h], :, h, :], km[s][r[h], :].rearrange("p (b h) -> p b h", b=NB)
                                                ).then_inc(*vec.mark("lm", a, s))
                        elif name == "ksum":
                            dve.wait_ge(*banks.ready(*use))
                            dve.tensor_scalar(km1[s][:], banks.of(*use)[:, 0:NB], 0.0, -ABSENT, ALU.is_equal, ALU.mult
                                              ).then_inc(*banks.drain(use, vec, "km1", a, s))
                            dve.wait_ge(*vec.at("km1", a, s))
                            k1 = km1[s][:].unsqueeze(2).broadcast_to((P, NB, 2))
                            dve.tensor_copy(km[s][:, 0:2 * NB].rearrange("p (b h) -> p b h", b=NB), k1
                                            ).then_inc(*vec.mark("km", a, s))
                            for h in range(2):
                                dve.tensor_copy(lm2[s][r[h], :, h, :],
                                                km1[s][r[h], :].unsqueeze(2).broadcast_to((64, NB, 2))
                                                ).then_inc(*vec.mark("lm", a, s))
                        elif name in ("maskrow", "maxrow"):
                            if name == "maxrow":
                                pairs = PAIRS[a]
                                dve.wait_ge(*vec.at("mx", a, s))
                                for h in range(2):
                                    dst = (nm8 if pairs == 8 else nm2)[s][r[h], :, h, :]
                                    src = mx[s][r[h], 0:NB * pairs].rearrange("p (b h) -> p b h", b=NB)
                                    dve.tensor_scalar(dst, src, -1.0, None, ALU.mult).then_inc(*vec.mark("nm", a, s))
                            dst, done = (lrow, "lrow") if name == "maskrow" else (mrow, "mrow")
                            dve.wait_ge(*banks.ready(*use))
                            n, m = (P, 8) if PAIRS[a] == 8 else (32, 16)
                            dve.tensor_tensor(dst[s][0:n, 0:m * S].rearrange("p (m t) -> p m t", m=m),
                                              banks.of(*use)[0:n, 0:S].unsqueeze(1).broadcast_to((n, m, S)),
                                              K32("own8" if m == 8 else "own2")[0:n, :].unsqueeze(2).broadcast_to(
                                                  (n, m, S)), ALU.mult).then_inc(*banks.drain(use, vec, done, a, s))
                        elif name in ("rowmax0", "rowmax1"):
                            for u in half_units(name, unit(a)[0]):
                                dve.wait_ge(*banks.ready("A", a, s, u))
                                dve.tensor_reduce(mx[s][:, 8 * u:8 * u + 8],
                                                  banks.of("A", a, s, u)[:].rearrange("p (h t) -> p h t", t=S),
                                                  AX.X, ALU.max).then_inc(*banks.drain(("A", a, s, u), vec, "mx", a, s))

                    def loop_unit(a, s, u):
                        if u == 0:
                            return
                        seqs = unit(a)[1]
                        heads = 2 * PAIRS[a]
                        dh = D // heads
                        done = [j for j in range(NT) if seqs * (u - 1) <= 2 * j + 1 < seqs * u]
                        for j in done:
                            t = banks.of("O", a, s, j)[:, 0:heads * (dh + 1)].rearrange("p (h d) -> p h d", h=heads)
                            dve.wait_ge(*banks.ready("O", a, s, j))
                            dve.reciprocal(rd[s][:, j % 2, 0:heads], t[:, :, dh]).then_inc(*vec.mark("rd", a, s, j))
                            dve.wait_ge(*vec.at("rd", a, s, j))
                            f = rd
                            if QUERYMASK[a]:
                                dve.tensor_scalar(rq[s][:, j % 2, 0:heads], rd[s][:, j % 2, 0:heads], qm[s][:, j:j + 1],
                                                  None, ALU.mult).then_inc(*vec.mark("rq", a, s, j))
                                dve.wait_ge(*vec.at("rq", a, s, j))
                                f = rq
                            dve.tensor_tensor(O[s][:, j, :].rearrange("p (h d) -> p h d", h=heads), t[:, :, 0:dh],
                                              f[s][:, j % 2, 0:heads].unsqueeze(2).broadcast_to((P, heads, dh)),
                                              ALU.mult).then_inc(*banks.drain(("O", a, s, j), vec, "O", a, s, j))

                    walk(loop_unit, step)

                @block.gpsimd
                def _(g_):
                    def deviation(sample, *tag):
                        s = tag[-1]
                        g_.wait_ge(*vec.at("mv", *tag))
                        if not sample:
                            g_.tensor_scalar(ve[s][:], mv[s][:, :, 1], 1e-5, None, ALU.add).then_inc(*pool.mark("ve", *tag))
                            g_.wait_ge(*pool.at("ve", *tag))
                            g_.tensor_tensor(rstd[s][:], ve[s][:], expo[:, 0, :], ALU.pow
                                             ).then_inc(*pool.mark("rstd", *tag))
                            return
                        g_.tensor_scalar(ve[s][:], mv[s][:, :, 1], D / (D - 1.0), None, ALU.mult
                                         ).then_inc(*pool.mark("ve", *tag))
                        g_.wait_ge(*pool.at("ve", *tag))
                        g_.tensor_tensor(dev[s][:], ve[s][:], expo[:, 1, :], ALU.pow).then_inc(*pool.mark("dev", *tag))
                        g_.wait_ge(*pool.at("dev", *tag))
                        g_.tensor_scalar(ve[s][:], dev[s][:], 1e-8, None, ALU.add).then_inc(*pool.mark("deve", *tag))
                        g_.wait_ge(*pool.at("deve", *tag))
                        g_.tensor_tensor(rstd[s][:], ve[s][:], expo[:, 2, :], ALU.pow).then_inc(*pool.mark("rstd", *tag))

                    def add_bias(name, a, s):
                        g_.tensor_tensor(X[s][:], X[s][:], rowb({("wo", 3): "bo2", ("w2", 3): "d2_b", ("w2", 5): "d4_b"}[
                            name, a]).unsqueeze(1).broadcast_to((P, NT, 128)), ALU.add
                            ).then_inc(*pool.mark("bias", name, a, s))

                    def step(name, a, s):
                        if name == "x1":
                            deviation(a >= 6, "x1", a, s)
                        elif name == "fc2":
                            deviation(False, "n3", a, s)
                        elif name == "q" or (name == "kv" and a == 2):
                            deviation(False, name, a, s)
                        elif name == "wo" and a == 3:
                            g_.wait_ge(*vec.at("q", 2, s))
                            add_bias(name, a, s)
                        elif name == "w2":
                            g_.wait_ge(*(banks.ready("x", 3, s) if a == 3 else vec.at("q", a, s)))
                            add_bias(name, a, s)
                        elif name == "ff":
                            g_.wait_ge(*vec.at("leaky", a, s))
                            g_.tensor_tensor(X[s][:], X[s][:], Y[s][:], ALU.add).then_inc(*pool.mark("enc", a, s))

                    walk(lambda a, s, u: None, step)

            nc.all_engine_barrier()
            nc.gpsimd.sem_clear(range(banks.filled[0].num, pool.sem.num + 1))
            nc.all_engine_barrier()
        return {"signals": {n: q.events for n, q in signals.items()},
                "banks": {"place": banks.place, "readers": banks.readers}}


def laid_out(v):
    L = "L%d_xattn_"
    heads = lambda w: w.transpose(1, 0, 2).reshape(D, D)
    down = lambda w: [w[128 * c:128 * c + 128] for c in range(4)]
    across = lambda w: [w[:, 128 * c:128 * c + 128] for c in range(4)]
    l0, l1, l2, l3 = ({k[len(L % i):]: a for k, a in v.items() if k.startswith(L % i)} for i in range(4))
    w = [heads(l0["Wq1"]), heads(l0["Wk1"]), heads(l0["Wv1"]), heads(l0["Wq2"]), heads(l0["Wk2"]), heads(l0["Wv2"]),
         l0["fc1_w"].T, l0["fc2_w"].T, l1["Wq"].T, l1["Wkv"][:D].T, l1["Wkv"][D:].T, l1["Wo"].T]
    w += across(l1["W1"].T) + down(l1["W2"].T)
    w += [l2["sa_w" + n] for n in "qkvo"] + [l2["ca_w" + n] for n in "qkvo"] + across(l2["ffn_w1"]) + down(l2["ffn_w2"])
    w += [l3[n][i] for i in range(3) for n in ("Wq", "Wk", "Wv", "Wff")]
    c = [l0["fc1_b"], l1["ln_q_g"], l1["ln_q_b"], l1["ln_kv_g"], l1["ln_kv_b"]] + list(l1["b1"].reshape(4, 128))
    c += [l2[f"ln{i}_{n}"] for i in (1, 2, 3) for n in "gb"] + list(l2["ffn_b1"].reshape(4, 128))
    c += list(l3["bq"]) + list(l3["bk"])
    r = [l0[f"ln{i}_{n}"] for i in (1, 2, 3) for n in "gb"] + [l0["fc2_b"], l1["bo"], l1["b2"], l2["ffn_b2"]]
    r += list(l3["gamma"]) + list(l3["beta"]) + list(l3["bv"]) + list(l3["bff"])
    return np.concatenate(w, 1), np.stack(c, 1), np.stack(r, 0)[None]


def kernel(**inputs):
    import concourse.bacc as bacc
    from concourse.bass_utils import run_bass_kernel_spmd

    v = {k: np.asarray(a) for k, a in inputs.items()}
    w, c, r = laid_out(v)
    k32, k16 = constants()
    k16 = k16.astype(mybir.dt.np(BF16))
    arrays = {"x": v["x"], "ctx": v["ctx_1024"], "weights": w, "columns": c, "rows": r, "const32": k32, "const16": k16}
    arrays = {n: np.ascontiguousarray(a) for n, a in arrays.items()}

    def build(known):
        nc = bacc.Bacc("TRN2", target_bir_lowering=False, num_devices=1)
        args = [nc.dram_tensor(n, a.shape, BF16 if n == "const16" else F32, kind="ExternalInput").ap()
                for n, a in arrays.items()]
        out = nc.dram_tensor("out", (SEQS, S, D), F32, kind="ExternalOutput").ap()
        return nc, network(nc, *args, out, known)

    _, known = build(None)
    nc, _ = build(known)
    result = run_bass_kernel_spmd(nc, [arrays], core_ids=[0])
    return result.results[0]["out"]
```

```python
from contextlib import ExitStack

import numpy as np

import concourse.bass as bass
from concourse import mybir

F32 = mybir.dt.float32
BF16 = mybir.dt.bfloat16
ACT = mybir.ActivationFunctionType
ALU = mybir.AluOpType
AX = mybir.AxisListType

P = 128
SEQS, S, D = 64, 64, 128
STREAMS = 4
NB = 4
NT = NB // 2
TOK = NB * S
GROUPS = SEQS // (STREAMS * NB)
BIG = 1.0e30
ABSENT = 4294967296.0 * 32.0 ** 0.5

ATTS = range(8)
PAIRS = [8, 8, 8, 8, 8, 2, 2, 2]
CAUSAL = [True, False, False, True, False, False, False, False]
KEYMASK = ["length", "length", None, None, None, "sum", "sum", "sum"]
QUERYMASK = [True, True, False, False, False, True, True, True]
KV_FROM = ["xf", "kf", "kf", "xf", "cf", "cf", "xf", "xf"]
BETWEEN = [
    "ctx _ x pv _ pq pk _ _ qpair0 qpair1 first length maskrow _ rowmax _ maxrow",
    "sum x1 _ kv pq | pk qpair0 qpair1 pv first | length maskrow rowmax maxrow _",
    "sum _ _ x1 fc1 _ fc2 n3 | _ q kvstats _ kv pq pk _ | qpair0 pv qpair1 rowmax _ _ maxrow _ _",
    "o wo x up0 up1 up2 | up3 down _ q pq pk | _ qpair0 pv qpair1 rowmax _ maxrow _ _",
    "o wo _ q _ | _ pq pk qpair0 pv | qpair1 rowmax _ maxrow _",
    "o wo _ q up0 up1 up2 | up3 _ down _ _ x pq pk qpair0 | pv qpair1 ksum _ maskrow rowmax maxrow _",
    "sum x1 _ ff x pq | pk qpair0 _ pv qpair1 | ksum maskrow rowmax maxrow",
    "sum _ _ _ _ x1 ff | x pq pk qpair0 pv qpair1 | ksum maskrow rowmax maxrow",
    "sum _ | x1 _ ff _ _ out | _",
]


def steps_before(a):
    return [lot.split() for lot in BETWEEN[a].split("|")]


WEIGHTS = (["wq0", "wk0", "wv0", "wq1", "wk1", "wv1", "fc1", "fc2", "wq2", "wk2", "wv2", "wo2"]
           + [f"u2_{c}" for c in range(4)] + [f"d2_{c}" for c in range(4)]
           + ["wq3", "wk3", "wv3", "wo3", "wq4", "wk4", "wv4", "wo4"]
           + [f"u4_{c}" for c in range(4)] + [f"d4_{c}" for c in range(4)]
           + [f"{w}{a}" for a in (5, 6, 7) for w in ("wq", "wk", "wv", "ff")])
COLUMNS = (["fc1_b", "q2_g", "q2_b", "kv2_g", "kv2_b"] + [f"u2_b{c}" for c in range(4)]
           + ["q3_g", "q3_b", "q4_g", "q4_b", "q5_g", "q5_b"] + [f"u4_b{c}" for c in range(4)]
           + ["bq5", "bq6", "bq7", "bk5", "bk6", "bk7"])
ROWS = ["n1_g", "n1_b", "n2_g", "n2_b", "n3_g", "n3_b", "fc2_b", "bo2", "d2_b", "d4_b",
        "e6_g", "e7_g", "e8_g", "e6_b", "e7_b", "e8_b", "bv5", "bv6", "bv7", "bff6", "bff7", "bff8"]
CONST32 = [("ident", 128), ("pair8", 8), ("pair2", 2), ("par8", 2), ("par2", 2), ("pos", 1), ("ones", 128),
           ("own8", 8), ("own2", 2 * NB)]
CONST16 = [("identb", 128), ("fold", 64), ("sel8", NB * 128), ("sel2", 128), ("samepar", 128),
           ("causB", 64), ("causA", 64), ("pairb8", 8 * S), ("pairb2", 2 * S)]


def constants():
    p = np.arange(P)
    eye = np.eye(P)
    c = {"ident": eye, "identb": eye, "ones": np.ones((P, 128)), "pos": (p % S)[:, None]}
    for n, pairs in (("8", 8), ("2", 2)):
        dh = D // (2 * pairs)
        c["pair" + n] = (p // (2 * dh))[:, None] == np.arange(pairs)
        c["pairb" + n] = np.repeat(c["pair" + n], S, axis=1)
        c["par" + n] = (p // dh % 2)[:, None] == np.arange(2)
    c["fold"] = (p % S)[:, None] == np.arange(S)
    parity = np.arange(P) // S
    c["own8"] = (p % 8)[:, None] == np.arange(8)
    c["sel8"] = ((p // 16)[:, None, None] == np.arange(NB)[None, :, None]) & \
        ((p // 8 % 2)[:, None, None] == parity[None, None, :])
    c["own2"] = ((p // 4)[:, None, None] == np.arange(NB)[None, :, None]) & ((p % 2)[:, None, None] == np.arange(2))
    c["sel2"] = (p // 2 % 2)[:, None] == parity[None, :]
    c["samepar"] = parity[:, None] == parity[None, :]
    c["causB"] = -BIG * ((p % S)[:, None] > np.arange(S)[None, :])
    c["causA"] = -BIG * (np.arange(S)[None, :] > (p % S)[:, None])
    flat = lambda names: np.concatenate([np.reshape(c[n], (P, w)).astype(np.float32) for n, w in names], 1)
    return flat(CONST32), flat(CONST16)


class Signal:

    def __init__(self, ctx, nc, name, known):
        self.sem = ctx.enter_context(nc.semaphore(name))
        self.name, self.known, self.count = name, known, 0
        self.events = {}

    def mark(self, *event, by=1):
        self.count += by
        self.events[event] = self.count
        return self.sem, by

    def at(self, *event):
        return self.sem, (self.known[self.name][event] if self.known else 1)


class Banks:

    def __init__(self, ctx, nc, known):
        self.filled = [ctx.enter_context(nc.semaphore(f"filled{k}")) for k in range(8)]
        self.tensor = [ctx.enter_context(nc.psum_tensor(f"bank{k}", [P, 512], F32)) for k in range(8)]
        self.known = known
        self.uses, self.readers, self.last, self.turn, self.place = [0] * 8, {}, {}, {}, {}

    def take(self, pe, ring, *use):
        n = self.turn[ring] = self.turn.get(ring, -1) + 1
        k = ring[n % len(ring)]
        if self.known and k in self.last:
            for sem, count in self.known["readers"][self.last[k]].items():
                pe.wait_ge(self.sems[sem], count)
        self.last[k] = use
        self.uses[k] += 1
        self.place[use] = (k, self.uses[k])
        return self.tensor[k]

    def full(self, *use):
        return self.filled[self.place[use][0]], 1

    def of(self, *use):
        return self.tensor[self.known["place"][use][0] if self.known else 0]

    def ready(self, *use):
        if not self.known:
            return self.filled[0], 1
        k, n = self.known["place"][use]
        return self.filled[k], n

    def drain(self, use, signal, *event):
        sem, by = signal.mark(*event)
        self.readers.setdefault(use, {})[signal.name] = signal.count
        return sem, by


NPT = 4
RING_S = (0, 1, 2)
RING_O = (3, 4)
RING_M = (5, 6, 7)


def network(nc, x, ctx_in, weights, columns, rows, const32, const16, out, known):
    x_g = x.rearrange("(i s j p) t d -> i s (p t) j d", i=GROUPS, s=STREAMS, p=2)
    c_g = ctx_in.rearrange("(i s j p) t d -> i s (p t) j d", i=GROUPS, s=STREAMS, p=2)
    o_g = out.rearrange("(i s j p) t d -> i s (p t) j d", i=GROUPS, s=STREAMS, p=2)

    with ExitStack() as ctx:
        def sb(name, shape, dt=F32):
            return ctx.enter_context(nc.sbuf_tensor(name, shape, dt))

        def per_stream(name, shape, dt=F32):
            return [sb(f"{name}{s}", shape, dt) for s in range(STREAMS)]

        W_all = sb("W_all", [P, len(WEIGHTS), 128])
        cols = sb("cols", [P, len(COLUMNS)])
        half = sb("half", [P, 4])
        bkpar = sb("bkpar", [P, 3, 2])
        row = sb("row", [P, len(ROWS), 128])
        c32 = sb("c32", [P, sum(w for _, w in CONST32)])
        c16 = sb("c16", [P, sum(w for _, w in CONST16)], BF16)

        def pick(buf, names, name):
            at = 0
            for n, w in names:
                if n == name:
                    return buf[:, at:at + w]
                at += w
            raise KeyError(name)

        def W(name):
            return W_all[:, WEIGHTS.index(name), :]

        def col(name):
            i = COLUMNS.index(name)
            return cols[:, i:i + 1]

        def rowb(name):
            return row[:, ROWS.index(name), :]

        def K32(name):
            return pick(c32, CONST32, name)

        def K16(name):
            return pick(c16, CONST16, name)

        X = per_stream("X", [P, NT, 128])
        C = per_stream("C", [P, NT, 128])
        Y = per_stream("Y", [P, NT, 128])
        Y2 = per_stream("Y2", [P, NT, 128])
        O = per_stream("O", [P, NT, 128])
        xf = per_stream("xf", [P, TOK])
        kf = per_stream("kf", [P, TOK])
        cf = per_stream("cf", [P, TOK])
        of = kf
        hid = per_stream("hid", [P, 4, TOK])
        tnh = per_stream("tnh", [P, 2, TOK])
        qs = per_stream("qs", [P, TOK])
        qb = per_stream("qb", [P, TOK], BF16)
        kb = per_stream("kb", [P, TOK], BF16)
        Qpar = per_stream("Qpar", [P, NB, 2, S], BF16)
        Kpar = per_stream("Kpar", [P, NB, 2, S])
        Qpair = per_stream("Qpair", [P, NB * 8 * S])
        Kpair = per_stream("Kpair", [P, NB * 8 * S], BF16)
        V8 = per_stream("V8", [P, NB, 8, 2, 9])
        V2 = per_stream("V2", [P, NB, 2, 2, 33])
        mx = per_stream("mx", [P, NB * 8])
        nm8 = per_stream("nm8", [P, NB, 2, 8], BF16)
        nm2 = per_stream("nm2", [P, NB, 2, 2], BF16)
        lm8 = per_stream("lm8", [P, NB, 2, 8], BF16)
        lm2 = per_stream("lm2", [P, NB, 2, 2], BF16)
        mrow = per_stream("mrow", [P, 512], BF16)
        lrow = per_stream("lrow", [P, 512], BF16)
        nz = per_stream("nz", [P, NB * 8], BF16)
        km = per_stream("km", [P, NB * 8], BF16)
        km1 = per_stream("km1", [P, NB])
        rd = per_stream("rd", [P, NT, 16])
        rq = per_stream("rq", [P, NT, 16])
        stats = per_stream("stats", [P, NT, 6])
        mv = per_stream("mv", [P, NT, 2])
        rstd = per_stream("rstd", [P, NT])
        ve = per_stream("ve", [P, NT])
        dev = per_stream("dev", [P, NT])
        am = per_stream("am", [P, NT])
        m0 = per_stream("m0", [P, NT])
        qm = per_stream("qm", [P, NT])
        PT = sb("PT", [P, NPT, 512])
        expo = sb("expo", [P, 3, NT])

        banks = Banks(ctx, nc, known and known["banks"])
        signals = {}

        def sig(name):
            if name not in signals:
                signals[name] = Signal(ctx, nc, name, known and known["signals"])
            return signals[name]

        setup = ctx.enter_context(nc.semaphore("setup"))
        setdve = ctx.enter_context(nc.semaphore("setdve"))
        loaded_w = ctx.enter_context(nc.semaphore("loaded_w"))

        x_in = [sig(f"x_in{s}") for s in range(STREAMS)]
        c_in = [sig(f"c_in{s}") for s in range(STREAMS)]
        x_out = [sig(f"x_out{s}") for s in range(STREAMS)]
        operand = sig("operand")
        probs = sig("probs")
        vec = sig("vec")
        pool = sig("pool")
        banks.sems = {n: signals[n].sem for n in signals}

        with nc.Block() as block:
            @block.sync
            def _(sp):
                sp.dma_start(c32[:], const32).then_inc(loaded_w, 16)
                sp.dma_start(c16[:], const16).then_inc(loaded_w, 16)
                sp.dma_start(cols[:], columns).then_inc(loaded_w, 16)
                sp.dma_start(W_all[:], weights.rearrange("p (n c) -> p n c", c=128)).then_inc(loaded_w, 16)
                sp.dma_start(row[:], rows.broadcast_to((P, len(ROWS), 128))).then_inc(loaded_w, 16)
                sp.wait_ge(loaded_w, 80)

            @block.gpsimd
            def _(g):
                n = 0
                for s in range(STREAMS):
                    for buf in (nm8, nm2, lm8, lm2, V8, V2):
                        g.memset(buf[s][:], 0.0).then_inc(setup, 1)
                        n += 1
                g.memset(expo[:, 0, :], -0.5).then_inc(setup, 1)
                g.memset(expo[:, 1, :], 0.5).then_inc(setup, 1)
                g.memset(expo[:, 2, :], -1.0).then_inc(setup, 1)
                g.wait_ge(setup, n + 3)
                for s in range(STREAMS):
                    for par in range(2):
                        rows_ = slice(64 * par, 64 * par + 64)
                        g.memset(V8[s][rows_, :, :, par, 8:9], 1.0).then_inc(setup, 1)
                        g.memset(V2[s][rows_, :, :, par, 32:33], 1.0).then_inc(setup, 1)
                g.wait_ge(setup, n + 3 + 8)

            @block.vector
            def _(v):
                v.wait_ge(loaded_w, 80)
                i = COLUMNS.index("u2_b0")
                v.tensor_scalar(half[:], cols[:, i:i + 4], 0.5, None, ALU.mult).then_inc(setdve, 1)
                for i in range(3):
                    v.tensor_scalar(bkpar[:, i, :], K32("par2"), col(f"bk{5 + i}"), None, ALU.mult
                                    ).then_inc(setdve, 1)
                v.wait_ge(setdve, 4)
        nc.all_engine_barrier()

        def unit(a):
            n = PAIRS[a] * S
            return NB * n // 512, 512 // n, n

        def tiles(ap):
            return ap.rearrange("p (j c) -> p j c", j=NT)

        def exp_number(a, s, u):
            return sum(STREAMS * unit(i)[0] for i in range(a)) + s * unit(a)[0] + u

        kv_of = lambda a, s: {"xf": xf, "kf": kf, "cf": cf}[KV_FROM[a]][s]

        def kv_event(a, s):
            if KV_FROM[a] == "cf":
                return "ctx", 0, s
            if KV_FROM[a] == "kf":
                return "kv", a, s
            return q_step(a), a, s

        def q_step(a):
            return {0: "x", 1: "x1", 2: "q", 3: "q", 4: "q", 5: "x", 6: "x", 7: "x"}[a]

        def walk(loop_unit, step):
            for name in steps_before(0)[0]:
                for s in range(STREAMS):
                    if name != "_":
                        step(name, 0, s)
            for a in ATTS:
                for s in range(STREAMS):
                    todo = []
                    for ago in range(1, STREAMS):
                        other = (s - ago) % STREAMS
                        before = a + 1 if other < s else a
                        if before > 0:
                            lot = steps_before(before)[ago - 1]
                            todo += [((i + 0.5) / len(lot), ago, name, before, other) for i, name in enumerate(lot)]
                    todo.sort()
                    units = unit(a)[0]
                    for u in range(units + 1):
                        loop_unit(a, s, u)
                        for _, _, name, before, other in todo[u * len(todo) // (units + 1):
                                                              (u + 1) * len(todo) // (units + 1)]:
                            if name != "_":
                                step(name, before, other)
            tail(step)

        def tail(step):
            lots = steps_before(len(ATTS))
            left = {s: sum(lots[STREAMS - 1 - s:], []) for s in range(STREAMS)}
            for i in range(max(len(steps) for steps in left.values())):
                for s in range(STREAMS):
                    if i < len(left[s]) and left[s][i] != "_":
                        step(left[s][i], len(ATTS), s)

        with nc.Fori(0, GROUPS) as g:
            with nc.Block() as block:
                @block.sync
                def _(sp):
                    for s in range(STREAMS):
                        sp.dma_start(C[s][:], c_g[g, s]).then_inc(*c_in[s].mark(by=16))
                        sp.dma_start(X[s][:], x_g[g, s]).then_inc(*x_in[s].mark(by=16))
                    for s in range(STREAMS):
                        sp.wait_ge(*pool.at("enc", 8, s))
                        sp.dma_start(o_g[g, s], X[s][:]).then_inc(*x_out[s].mark(by=16))
                    for s in range(STREAMS):
                        sp.wait_ge(*x_out[s].at())

                @block.tensor
                def _(pe):
                    def turn(src, use):
                        t = banks.take(pe, RING_M, *use)
                        for j in range(NT):
                            mm = pe.transpose(t[:, 128 * j:128 * j + 128], src[:, j, :], K32("ident"))
                        mm.then_inc(*banks.full(*use))

                    def token_major(src, name, use):
                        t = banks.take(pe, RING_M, *use)
                        for j in range(NT):
                            mm = pe.matmul(t[:, 128 * j:128 * j + 128], src[:, 128 * j:128 * j + 128], W(name),
                                           start=True, stop=True)
                        mm.then_inc(*banks.full(*use))

                    def feature_major(src, name, use):
                        t = banks.take(pe, RING_M, *use)
                        pe.matmul(t[:, 0:TOK], W(name), src[:], start=True, stop=True).then_inc(*banks.full(*use))

                    def step(name, a, s):
                        use = (name, a, s)
                        if name == "ctx":
                            pe.wait_ge(*c_in[s].at())
                            turn(C[s], use)
                        elif name == "x":
                            if a == 0:
                                pe.wait_ge(*x_in[s].at())
                            elif a in (3, 5):
                                pe.wait_ge(*vec.at("wo" if a == 3 else "down", a, s))
                            else:
                                pe.wait_ge(*pool.at("enc", a, s))
                            turn(X[s], use)
                        elif name == "x1":
                            pe.wait_ge(*vec.at("x1", a, s))
                            turn(X[s], use)
                        elif name == "q":
                            pe.wait_ge(*vec.at("q", a, s))
                            turn(Y[s], use)
                        elif name == "kv":
                            pe.wait_ge(*vec.at("kv", a, s))
                            turn(Y2[s], use)
                        elif name == "fc1":
                            pe.wait_ge(*operand.at("x1", a, s))
                            feature_major(xf[s], "fc1", use)
                        elif name == "fc2":
                            pe.wait_ge(*operand.at("fc1", a, s))
                            token_major(hid[s][:, 0, :], "fc2", use)
                        elif name == "o":
                            pe.wait_ge(*vec.at("O", a - 1, s))
                            turn(O[s], use)
                        elif name == "wo":
                            pe.wait_ge(*operand.at("o", a, s))
                            token_major(of[s], f"wo{a - 1}", use)
                        elif name[:2] == "up":
                            pe.wait_ge(*operand.at("x" if a == 3 else "q", a, s))
                            feature_major(xf[s], f"u{a - 1}_{name[2]}", use)
                        elif name == "down":
                            pe.wait_ge(*(vec if a == 3 else operand).at("up3", a, s))
                            t = banks.take(pe, RING_M, *use)
                            for j in range(NT):
                                for c in range(4):
                                    mm = pe.matmul(t[:, 128 * j:128 * j + 128], hid[s][:, c, 128 * j:128 * j + 128],
                                                   W(f"d{a - 1}_{c}"), start=c == 0, stop=c == 3)
                            mm.then_inc(*banks.full(*use))
                        elif name == "ff":
                            pe.wait_ge(*operand.at("x1", a, s))
                            t = banks.take(pe, RING_M, *use)
                            for j in range(NT):
                                out_j = t[:, 128 * j:128 * j + 128]
                                pe.matmul(out_j, xf[s][:, 128 * j:128 * j + 128], W(f"ff{a - 1}"),
                                          start=True, stop=False)
                                mm = pe.matmul(out_j, K32("ones")[0:1, :], rowb(f"bff{a}")[0:1, :],
                                               start=False, stop=True)
                            mm.then_inc(*banks.full(*use))
                        elif name == "pk":
                            pe.wait_ge(*operand.at(*kv_event(a, s)))
                            feature_major(kv_of(a, s), f"wk{a}", use)
                        elif name == "pq":
                            pe.wait_ge(*operand.at(q_step(a), a, s))
                            feature_major(xf[s], f"wq{a}", use)
                        elif name == "pv":
                            src, pairs = kv_of(a, s), PAIRS[a]
                            t = banks.take(pe, RING_M, *use)
                            w = W(f"wv{a}").rearrange("p (h r d) -> p h r d", h=pairs, r=2)
                            for b in range(NB):
                                for par in range(2):
                                    out_b = t[64 * par:64 * par + 64, S * b:S * b + S]
                                    mm = pe.matmul(out_b, src[:, S * b:S * b + S], w[:, :, par, :],
                                                   start=True, stop=pairs == 8)
                                    if pairs == 2:
                                        bias = rowb(f"bv{a}")[0:1, :].rearrange("p (h r d) -> p h r d", h=2, r=2)
                                        mm = pe.matmul(out_b, K32("ones")[0:1, 0:64], bias[:, :, par, :],
                                                       start=False, stop=True)
                            mm.then_inc(*banks.full(*use))
                        elif name == "first":
                            pe.wait_ge(*operand.at("qpair1", a, s))
                            pe.wait_ge(*operand.at("pk", a, s))
                            t = banks.take(pe, RING_M, *use)
                            q = Qpair[s].rearrange("p (b h q) -> p b h q", b=NB, q=S)
                            for b in range(NB):
                                mm = pe.matmul(t[:, 8 * b:8 * b + 8], Kpar[s][:, b].rearrange("p r t -> p (r t)"), q[:, b, :, 0],
                                               start=True, stop=True)
                            mm.then_inc(*banks.full(*use))
                        elif name == "length":
                            pe.wait_ge(*vec.at("nz", a, s))
                            t = banks.take(pe, RING_M, *use)
                            pe.matmul(t[:, 0:NB * 8], K16("samepar"), nz[s][:], start=True, stop=True
                                      ).then_inc(*banks.full(*use))
                        elif name == "ksum":
                            t = banks.take(pe, RING_M, *use)
                            src = kv_of(a, s)
                            for b in range(NB):
                                for r in (0, 64):
                                    mm = pe.matmul(t[r:r + 64, b:b + 1], src[:, S * b:S * b + S], K32("ones")[:, 0:1],
                                                   start=True, stop=True)
                            mm.then_inc(*banks.full(*use))
                        elif name in ("maskrow", "maxrow"):
                            pe.wait_ge(*vec.at("lm" if name == "maskrow" else "nm", a, s))
                            t = banks.take(pe, RING_M, *use)
                            m = {("maskrow", 8): lm8, ("maskrow", 2): lm2, ("maxrow", 8): nm8, ("maxrow", 2): nm2}[
                                name, PAIRS[a]][s]
                            n = NB * 2 * PAIRS[a]
                            pe.matmul(t[0:n, 0:S], m.rearrange("p b r h -> p (b r h)"), K16("fold"),
                                      start=True, stop=True).then_inc(*banks.full(*use))
                        elif name == "rowmax":
                            units = unit(a)[0]
                            pe.wait_ge(*vec.at("Kpair", a, s))
                            pe.wait_ge(*vec.at("Qpar", a, s))
                            if KEYMASK[a]:
                                pe.wait_ge(*vec.at("lrow", a, s))
                            for u in range(units):
                                scores("A", a, s, u, Qpar[s], Kpair[s])

                    def mask_terms(kind, a, s, u):
                        seqs, pairs = unit(a)[1], PAIRS[a]
                        terms = []
                        if CAUSAL[a]:
                            terms.append((K16("identb"), K16("caus" + kind).unsqueeze(1).broadcast_to((P, 8, S))))
                        if kind == "B" and KEYMASK[a]:
                            m = km[s][:, 8 * u:8 * u + 8]
                            terms.append((K16("identb"), m.unsqueeze(2).broadcast_to((P, 8, S))))
                        spread = [lrow] if kind == "A" and KEYMASK[a] else [mrow] if kind == "B" else []
                        for r in spread:
                            if pairs == 8:
                                sel = K16("sel8").rearrange("p (b c) -> p b c", b=NB)[0:16 * NB, u, :]
                                terms.append((sel, r[s][0:16 * NB, :]))
                            else:
                                terms.append((K16("sel2")[0:4 * NB, :], r[s][0:4 * NB, :]))
                        return terms

                    def scores(kind, a, s, u, stationary, moving):
                        units, seqs, n = unit(a)
                        t = banks.take(pe, RING_S, kind, a, s, u)
                        terms = mask_terms(kind, a, s, u)
                        m = moving[:, 0:NB * n].rearrange("p (b c) -> p b c", b=NB)
                        for i in range(seqs):
                            b = seqs * u + i
                            mm = pe.matmul(t[:, n * i:n * i + n], stationary[:, b].rearrange("p r t -> p (r t)"),
                                           m[:, b, :], start=i == 0,
                                           stop=i == seqs - 1 and not terms, skip_group_check=True)
                        for i, (fixed, spread) in enumerate(terms):
                            mm = pe.matmul(t[:], fixed, spread, start=False, stop=i == len(terms) - 1,
                                           skip_group_check=True)
                        mm.then_inc(*banks.full(kind, a, s, u))

                    def values(a, s, u):
                        units, seqs, n = unit(a)
                        pairs = PAIRS[a]
                        w = 2 * (D // (2 * pairs) + 1)
                        V = (V8 if pairs == 8 else V2)[s]
                        pe.wait_ge(*probs.at(a, s, u))
                        if u == 0:
                            pe.wait_ge(*operand.at("V", a, s))
                        p = PT[:, exp_number(a, s, u) % NPT, :].rearrange("p (b h q) -> p b h q", h=pairs, q=S)
                        for i in range(seqs):
                            b = seqs * u + i
                            if b == 0:
                                outputs[0] = banks.take(pe, RING_O, "O", a, s)
                            r = slice(64 * (b % 2), 64 * (b % 2) + 64)
                            for h in range(pairs):
                                at = w * (pairs * (b // 2) + h)
                                mm = pe.matmul(outputs[0][r, at:at + w], p[:, i, h, :],
                                               V[:, b, h].rearrange("p r d -> p (r d)"), start=True, stop=True)
                            if b == NB - 1:
                                mm.then_inc(*banks.full("O", a, s))

                    outputs = [None]

                    def loop_unit(a, s, u):
                        if u < unit(a)[0]:
                            if u == 0:
                                pe.wait_ge(*operand.at("qpair1", a, s))
                                pe.wait_ge(*operand.at("pk", a, s))
                                pe.wait_ge(*vec.at("mrow", a, s))
                            scores("B", a, s, u, Kpar[s], Qpair[s])
                        if u >= 1:
                            values(a, s, u - 1)

                    walk(loop_unit, step)

                @block.scalar
                def _(act):
                    def move(dst, src, use, *event, f=ACT.Copy, **kw):
                        act.wait_ge(*banks.ready(*use))
                        act.activation(dst, src, f, **kw).then_inc(*banks.drain(use, operand, *event))

                    def step(name, a, s):
                        use = (name, a, s)
                        full = banks.of(*use)[:, 0:TOK] if name in (
                            "ctx", "x", "x1", "q", "kv", "fc1", "o", "ff", "pk", "pq", "pv", "up0", "up1", "up2", "up3"
                        ) else None
                        if name == "ctx":
                            move(cf[s][:], full, use, *use)
                        elif name in ("x", "x1"):
                            move(xf[s][:], full, use, *use)
                        elif name == "q":
                            move(xf[s][:], full, use, *use, f=ACT.Identity, scale=col(f"q{a}_g"), bias=col(f"q{a}_b"))
                        elif name == "kv" and a == 1:
                            move(kf[s][:], full, use, *use)
                        elif name == "kv":
                            move(kf[s][:], full, use, *use, f=ACT.Identity, scale=col("kv2_g"), bias=col("kv2_b"))
                        elif name == "fc1":
                            move(hid[s][:, 0, :], full, use, *use, f=ACT.Relu, bias=col("fc1_b"))
                        elif name == "o":
                            move(of[s][:], full, use, *use)
                        elif name[:2] == "up" and a == 3:
                            c = int(name[2])
                            if c >= 2:
                                act.wait_ge(*vec.at("part", f"up{c - 2}", a, s))
                            move(tnh[s][:, c % 2, :], full, use, "tanh", *use, f=ACT.Tanh, scale=0.5,
                                 bias=half[:, c:c + 1])
                        elif name[:2] == "up":
                            move(hid[s][:, int(name[2]), :], full, use, *use, f=ACT.Relu, bias=col(f"u4_b{name[2]}"))
                        elif name == "ff":
                            move(Y[s].rearrange("p j c -> p (j c)"), full, use, "fifth", a, s, scale=0.2)
                        elif name == "pq":
                            kw = {"f": ACT.Relu, "bias": col(f"bq{a}")} if PAIRS[a] == 2 else {}
                            move(qb[s][:], full, use, *use, **kw)
                            move(qs[s][:], full, use, "qs", a, s, **kw)
                        elif name == "pk":
                            kw = {"f": ACT.Relu, "bias": col(f"bk{a}")} if PAIRS[a] == 2 else {}
                            move(kb[s][:], full, use, "pkb", a, s, **kw)
                            for h in range(2):
                                if PAIRS[a] == 2:
                                    kw["bias"] = bkpar[:, a - 5, h:h + 1]
                                move(Kpar[s][:, :, h, :], full.rearrange("p (b t) -> p b t", b=NB), use, *use,
                                     scale=K32(f"par{PAIRS[a]}")[:, h:h + 1], **kw)
                        elif name in ("qpair0", "qpair1"):
                            pairs = PAIRS[a]
                            d = Qpair[s][:, 0:NB * pairs * S].rearrange("p (b h t) -> p b h t", b=NB, h=pairs)
                            half_ = range(pairs // 2) if name == "qpair0" else range(pairs // 2, pairs)
                            act.wait_ge(*operand.at("qs", a, s))
                            for h in half_:
                                act.activation(d[:, :, h, :], qs[s].rearrange("p (b t) -> p b t", b=NB), ACT.Copy,
                                               scale=K32(f"pair{pairs}")[:, h:h + 1]).then_inc(*operand.mark(*use))
                        elif name == "pv":
                            pairs = PAIRS[a]
                            dh = D // (2 * pairs)
                            V = (V8 if pairs == 8 else V2)[s]
                            t = full.rearrange("p (b h d) -> p b h d", b=NB, h=pairs)
                            for par in range(2):
                                r = slice(64 * par, 64 * par + 64)
                                move(V[r, :, :, par, 0:dh], t[r], use, *(("V", a, s) if par else ("V0", a, s)),
                                     f=ACT.Relu if pairs == 2 else ACT.Copy)

                    def loop_unit(a, s, u):
                        if u == unit(a)[0]:
                            return
                        n = exp_number(a, s, u)
                        if n >= NPT:
                            act.wait_ge(*banks.ready("O", *exp_user[n - NPT]))
                        act.wait_ge(*banks.ready("B", a, s, u))
                        act.activation(PT[:, n % NPT, :], banks.of("B", a, s, u)[:], ACT.Exp,
                                       scale=float((D // (2 * PAIRS[a])) ** -0.5)
                                       ).then_inc(*banks.drain(("B", a, s, u), probs, a, s, u))

                    exp_user = {exp_number(a, s, u): (a, s)
                                for a in ATTS for s in range(STREAMS) for u in range(unit(a)[0])}
                    walk(loop_unit, step)

                @block.vector
                def _(dve):
                    def moments(src, *tag):
                        for j in range(NT):
                            dve.bn_stats(stats[tag[-1]][:, j, :], src[:, j, :]).then_inc(*vec.mark("stats", *tag))
                        dve.wait_ge(*vec.at("stats", *tag))
                        for j in range(NT):
                            dve.bn_aggr(mv[tag[-1]][:, j, :], stats[tag[-1]][:, j, :]).then_inc(*vec.mark("mv", *tag))

                    def norm(dst, src, *tag):
                        s = tag[-1]
                        dve.wait_ge(*pool.at("rstd", *tag))
                        for j in range(NT):
                            dve.tensor_scalar(dst[:, j, :], src[:, j, :], mv[s][:, j, 0:1], rstd[s][:, j:j + 1],
                                              ALU.subtract, ALU.mult).then_inc(*vec.mark(*tag))

                    def norm_affine(name, *tag):
                        s = tag[-1]
                        dve.wait_ge(*pool.at("rstd", *tag))
                        for j in range(NT):
                            dve.scalar_tensor_tensor(out=Y[s][:, j, :], in0=X[s][:, j, :], scalar=mv[s][:, j, 0:1],
                                                     in1=rowb(name + "_g"), op0=ALU.subtract, op1=ALU.mult
                                                     ).then_inc(*vec.mark("scaled", *tag))
                        dve.wait_ge(*vec.at("scaled", *tag))
                        for j in range(NT):
                            dve.scalar_tensor_tensor(out=X[s][:, j, :], in0=Y[s][:, j, :], scalar=rstd[s][:, j:j + 1],
                                                     in1=rowb(name + "_b"), op0=ALU.mult, op1=ALU.add
                                                     ).then_inc(*vec.mark(*tag))

                    def present(a, s, op, absolute):
                        dve.tensor_reduce(am[s][:], X[s][:], AX.X, op, apply_absolute_value=absolute
                                          ).then_inc(*vec.mark("am", a, s))
                        dve.wait_ge(*vec.at("am", a, s))
                        dve.tensor_scalar(qm[s][:], am[s][:], 0.0, None, ALU.not_equal).then_inc(*vec.mark("qm", a, s))

                    def step(name, a, s):
                        use = (name, a, s)
                        r = [slice(0, 64), slice(64, 128)]
                        if name == "x":
                            if a == 0:
                                dve.wait_ge(*x_in[s].at())
                                present(a, s, ALU.max, True)
                                dve.wait_ge(*vec.at("qm", a, s))
                                dve.tensor_copy(m0[s][:], qm[s][:]).then_inc(*vec.mark("m0", s))
                            elif a >= 5:
                                dve.wait_ge(*(vec.at("down", 5, s) if a == 5 else pool.at("enc", a, s)))
                                present(a, s, ALU.add, False)
                        elif name == "sum":
                            dve.wait_ge(*vec.at("O", a - 1, s))
                            dve.tensor_tensor(X[s][:], X[s][:], O[s][:], ALU.add).then_inc(*vec.mark("sum", a, s))
                            dve.wait_ge(*vec.at("sum", a, s))
                            moments(X[s], "x1", a, s)
                        elif name == "x1":
                            norm_affine(f"n{a}" if a < 3 else f"e{a}", "x1", a, s)
                            if a == 1:
                                dve.wait_ge(*vec.at("x1", a, s))
                                present(a, s, ALU.max, True)
                        elif name == "kv" and a == 1:
                            dve.wait_ge(*c_in[s].at())
                            dve.wait_ge(*vec.at("qm", a, s))
                            for j in range(NT):
                                dve.tensor_scalar(Y2[s][:, j, :], C[s][:, j, :], qm[s][:, j:j + 1], None, ALU.mult
                                                  ).then_inc(*vec.mark(*use))
                        elif name == "kvstats":
                            moments(C[s], "kv", a, s)
                        elif name == "kv":
                            dve.wait_ge(*banks.ready("kv", 1, s))
                            norm(Y2[s], C[s], *use)
                        elif name == "q":
                            norm(Y[s], X[s], *use)
                        elif name == "fc2":
                            dve.wait_ge(*banks.ready(*use))
                            dve.tensor_tensor(Y[s][:], tiles(banks.of(*use)[:, 0:TOK]),
                                              rowb("fc2_b").unsqueeze(1).broadcast_to((P, NT, 128)), ALU.add
                                              ).then_inc(*banks.drain(use, vec, "z", a, s))
                            dve.wait_ge(*vec.at("z", a, s))
                            for j in range(NT):
                                dve.scalar_tensor_tensor(out=X[s][:, j, :], in0=Y[s][:, j, :], scalar=m0[s][:, j:j + 1],
                                                         in1=X[s][:, j, :], op0=ALU.mult, op1=ALU.add
                                                         ).then_inc(*vec.mark("x2", a, s))
                            dve.wait_ge(*vec.at("x2", a, s))
                            moments(X[s], "n3", a, s)
                        elif name == "n3":
                            norm_affine("n3", "n3", a, s)
                            dve.wait_ge(*vec.at("n3", a, s))
                            moments(X[s], "q", a, s)
                        elif name in ("wo", "down"):
                            if a == 3 or name == "down":
                                dve.wait_ge(*pool.at("bias", name, a, s))
                            dve.wait_ge(*banks.ready(*use))
                            dve.scalar_tensor_tensor(out=X[s].rearrange("p j c -> p (j c)"), in0=banks.of(*use)[:, 0:TOK],
                                                     scalar=0.5 if use[:2] == ("down", 3) else 1.0,
                                                     in1=X[s].rearrange("p j c -> p (j c)"), op0=ALU.mult, op1=ALU.add
                                                     ).then_inc(*banks.drain(use, vec, *use))
                            if (name, a) in (("down", 3), ("wo", 4), ("wo", 5)):
                                dve.wait_ge(*vec.at(*use))
                                moments(X[s], "q", a, s)
                        elif name == "ff":
                            dve.wait_ge(*operand.at("fifth", a, s))
                            y = Y[s].rearrange("p j c -> p (j c)")
                            dve.scalar_tensor_tensor(out=y, in0=banks.of(*use)[:, 0:TOK], scalar=1.0, in1=y, op0=ALU.mult,
                                                     op1=ALU.max).then_inc(*banks.drain(use, vec, "leaky", a, s))
                        elif name[:2] == "up" and a == 3:
                            c = int(name[2])
                            t = banks.of(*use)[:, 0:TOK]
                            dve.wait_ge(*operand.at("tanh", *use))
                            dve.scalar_tensor_tensor(out=hid[s][:, c, :], in0=t, scalar=col(f"u2_b{c}"),
                                                     in1=tnh[s][:, c % 2, :], op0=ALU.add, op1=ALU.mult
                                                     ).then_inc(*vec.mark("part", *use))
                            dve.wait_ge(*vec.at("part", *use))
                            dve.scalar_tensor_tensor(out=hid[s][:, c, :], in0=t, scalar=col(f"u2_b{c}"),
                                                     in1=hid[s][:, c, :], op0=ALU.add, op1=ALU.add
                                                     ).then_inc(*banks.drain(use, vec, *use))
                        elif name == "pq":
                            dve.wait_ge(*operand.at(*use))
                            for h in range(2):
                                dve.tensor_scalar(Qpar[s][:, :, h, :], qb[s].rearrange("p (b t) -> p b t", b=NB),
                                                  K32(f"par{PAIRS[a]}")[:, h:h + 1], None, ALU.mult
                                                  ).then_inc(*vec.mark("Qpar", a, s))
                        elif name == "pk":
                            pairs = PAIRS[a]
                            dve.wait_ge(*operand.at("pkb", a, s))
                            dve.tensor_tensor(Kpair[s][:, 0:NB * pairs * S].rearrange("p (b h t) -> p b h t", b=NB, h=pairs),
                                              kb[s].rearrange("p (b t) -> p b t", b=NB).unsqueeze(2).broadcast_to(
                                                  (P, NB, pairs, S)),
                                              K16(f"pairb{pairs}").rearrange("p (h t) -> p h t", h=pairs).unsqueeze(1)
                                              .broadcast_to((P, NB, pairs, S)), ALU.mult
                                              ).then_inc(*vec.mark("Kpair", a, s))
                        elif name == "first":
                            dve.wait_ge(*banks.ready(*use))
                            dve.tensor_scalar(nz[s][:], banks.of(*use)[:, 0:8 * NB], 0.0, None, ALU.not_equal
                                              ).then_inc(*banks.drain(use, vec, "nz", a, s))
                        elif name == "length":
                            dve.wait_ge(*banks.ready(*use))
                            dve.tensor_scalar(km[s][:], banks.of(*use)[:, 0:8 * NB], K32("pos"), -BIG, ALU.is_le, ALU.mult
                                              ).then_inc(*banks.drain(use, vec, "km", a, s))
                            dve.wait_ge(*vec.at("km", a, s))
                            for h in range(2):
                                dve.tensor_copy(lm8[s][r[h], :, h, :], km[s][r[h], :].rearrange("p (b h) -> p b h", b=NB)
                                                ).then_inc(*vec.mark("lm", a, s))
                        elif name == "ksum":
                            dve.wait_ge(*banks.ready(*use))
                            dve.tensor_scalar(km1[s][:], banks.of(*use)[:, 0:NB], 0.0, -ABSENT, ALU.is_equal, ALU.mult
                                              ).then_inc(*banks.drain(use, vec, "km1", a, s))
                            dve.wait_ge(*vec.at("km1", a, s))
                            k1 = km1[s][:].unsqueeze(2).broadcast_to((P, NB, 2))
                            dve.tensor_copy(km[s][:, 0:2 * NB].rearrange("p (b h) -> p b h", b=NB), k1
                                            ).then_inc(*vec.mark("km", a, s))
                            for h in range(2):
                                dve.tensor_copy(lm2[s][r[h], :, h, :],
                                                km1[s][r[h], :].unsqueeze(2).broadcast_to((64, NB, 2))
                                                ).then_inc(*vec.mark("lm", a, s))
                        elif name in ("maskrow", "maxrow"):
                            if name == "maxrow":
                                pairs = PAIRS[a]
                                dve.wait_ge(*vec.at("mx", a, s))
                                for h in range(2):
                                    dst = (nm8 if pairs == 8 else nm2)[s][r[h], :, h, :]
                                    src = mx[s][r[h], 0:NB * pairs].rearrange("p (b h) -> p b h", b=NB)
                                    dve.tensor_scalar(dst, src, -1.0, None, ALU.mult).then_inc(*vec.mark("nm", a, s))
                            dst, done = (lrow, "lrow") if name == "maskrow" else (mrow, "mrow")
                            dve.wait_ge(*banks.ready(*use))
                            n, m = (16 * NB, 8) if PAIRS[a] == 8 else (4 * NB, 2 * NB)
                            dve.tensor_tensor(dst[s][0:n, 0:m * S].rearrange("p (m t) -> p m t", m=m),
                                              banks.of(*use)[0:n, 0:S].unsqueeze(1).broadcast_to((n, m, S)),
                                              K32(f"own{PAIRS[a]}")[0:n, :].unsqueeze(2).broadcast_to(
                                                  (n, m, S)), ALU.mult).then_inc(*banks.drain(use, vec, done, a, s))
                        elif name == "rowmax":
                            for u in range(unit(a)[0]):
                                dve.wait_ge(*banks.ready("A", a, s, u))
                                dve.tensor_reduce(mx[s][:, 8 * u:8 * u + 8],
                                                  banks.of("A", a, s, u)[:].rearrange("p (h t) -> p h t", t=S),
                                                  AX.X, ALU.max).then_inc(*banks.drain(("A", a, s, u), vec, "mx", a, s))

                    def loop_unit(a, s, u):
                        if u < unit(a)[0]:
                            return
                        heads = 2 * PAIRS[a]
                        dh = D // heads
                        t = banks.of("O", a, s)[:, 0:NT * heads * (dh + 1)].rearrange(
                            "p (j h d) -> p j h d", j=NT, h=heads)
                        dve.wait_ge(*banks.ready("O", a, s))
                        dve.reciprocal(rd[s][:, :, 0:heads], t[:, :, :, dh]).then_inc(*vec.mark("rd", a, s))
                        dve.wait_ge(*vec.at("rd", a, s))
                        f = rd
                        if QUERYMASK[a]:
                            dve.tensor_tensor(rq[s][:, :, 0:heads], rd[s][:, :, 0:heads],
                                              qm[s][:].unsqueeze(2).broadcast_to((P, NT, heads)), ALU.mult
                                              ).then_inc(*vec.mark("rq", a, s))
                            dve.wait_ge(*vec.at("rq", a, s))
                            f = rq
                        dve.tensor_tensor(O[s].rearrange("p j (h d) -> p j h d", h=heads), t[:, :, :, 0:dh],
                                          f[s][:, :, 0:heads].unsqueeze(3).broadcast_to((P, NT, heads, dh)),
                                          ALU.mult).then_inc(*banks.drain(("O", a, s), vec, "O", a, s))

                    walk(loop_unit, step)

                @block.gpsimd
                def _(g_):
                    def deviation(sample, *tag):
                        s = tag[-1]
                        g_.wait_ge(*vec.at("mv", *tag))
                        if not sample:
                            g_.tensor_scalar(ve[s][:], mv[s][:, :, 1], 1e-5, None, ALU.add).then_inc(*pool.mark("ve", *tag))
                            g_.wait_ge(*pool.at("ve", *tag))
                            g_.tensor_tensor(rstd[s][:], ve[s][:], expo[:, 0, :], ALU.pow
                                             ).then_inc(*pool.mark("rstd", *tag))
                            return
                        g_.tensor_scalar(ve[s][:], mv[s][:, :, 1], D / (D - 1.0), None, ALU.mult
                                         ).then_inc(*pool.mark("ve", *tag))
                        g_.wait_ge(*pool.at("ve", *tag))
                        g_.tensor_tensor(dev[s][:], ve[s][:], expo[:, 1, :], ALU.pow).then_inc(*pool.mark("dev", *tag))
                        g_.wait_ge(*pool.at("dev", *tag))
                        g_.tensor_scalar(ve[s][:], dev[s][:], 1e-8, None, ALU.add).then_inc(*pool.mark("deve", *tag))
                        g_.wait_ge(*pool.at("deve", *tag))
                        g_.tensor_tensor(rstd[s][:], ve[s][:], expo[:, 2, :], ALU.pow).then_inc(*pool.mark("rstd", *tag))

                    def add_bias(name, a, s):
                        g_.tensor_tensor(X[s][:], X[s][:], rowb({("wo", 3): "bo2", ("down", 3): "d2_b", ("down", 5): "d4_b"}[
                            name, a]).unsqueeze(1).broadcast_to((P, NT, 128)), ALU.add
                            ).then_inc(*pool.mark("bias", name, a, s))

                    def step(name, a, s):
                        if name == "sum":
                            deviation(a >= 6, "x1", a, s)
                        elif name == "fc2":
                            deviation(False, "n3", a, s)
                        elif name == "kvstats":
                            deviation(False, "kv", a, s)
                        elif name == "n3" or (name == "wo" and a > 3):
                            deviation(False, "q", a, s)
                        elif name == "wo" and a == 3:
                            g_.wait_ge(*vec.at("q", 2, s))
                            add_bias(name, a, s)
                        elif name == "down":
                            g_.wait_ge(*(banks.ready("x", 3, s) if a == 3 else vec.at("q", a, s)))
                            add_bias(name, a, s)
                            if a == 3:
                                deviation(False, "q", a, s)
                        elif name == "ff":
                            g_.wait_ge(*vec.at("leaky", a, s))
                            g_.tensor_tensor(X[s][:], X[s][:], Y[s][:], ALU.add).then_inc(*pool.mark("enc", a, s))

                    walk(lambda a, s, u: None, step)

            nc.all_engine_barrier()
            nc.gpsimd.sem_clear(range(banks.filled[0].num, pool.sem.num + 1))
            nc.all_engine_barrier()
        return {"signals": {n: q.events for n, q in signals.items()},
                "banks": {"place": banks.place, "readers": banks.readers}}


def laid_out(v):
    L = "L%d_xattn_"
    heads = lambda w: w.transpose(1, 0, 2).reshape(D, D)
    down = lambda w: [w[128 * c:128 * c + 128] for c in range(4)]
    across = lambda w: [w[:, 128 * c:128 * c + 128] for c in range(4)]
    l0, l1, l2, l3 = ({k[len(L % i):]: a for k, a in v.items() if k.startswith(L % i)} for i in range(4))
    w = [heads(l0["Wq1"]), heads(l0["Wk1"]), heads(l0["Wv1"]), heads(l0["Wq2"]), heads(l0["Wk2"]), heads(l0["Wv2"]),
         l0["fc1_w"].T, l0["fc2_w"].T, l1["Wq"].T, l1["Wkv"][:D].T, l1["Wkv"][D:].T, l1["Wo"].T]
    w += across(l1["W1"].T) + down(l1["W2"].T)
    w += [l2["sa_w" + n] for n in "qkvo"] + [l2["ca_w" + n] for n in "qkvo"] + across(l2["ffn_w1"]) + down(l2["ffn_w2"])
    w += [l3[n][i] for i in range(3) for n in ("Wq", "Wk", "Wv", "Wff")]
    c = [l0["fc1_b"], l1["ln_q_g"], l1["ln_q_b"], l1["ln_kv_g"], l1["ln_kv_b"]] + list(l1["b1"].reshape(4, 128))
    c += [l2[f"ln{i}_{n}"] for i in (1, 2, 3) for n in "gb"] + list(l2["ffn_b1"].reshape(4, 128))
    c += list(l3["bq"]) + list(l3["bk"])
    r = [l0[f"ln{i}_{n}"] for i in (1, 2, 3) for n in "gb"] + [l0["fc2_b"], l1["bo"], l1["b2"], l2["ffn_b2"]]
    r += list(l3["gamma"]) + list(l3["beta"]) + list(l3["bv"]) + list(l3["bff"])
    return np.concatenate(w, 1), np.stack(c, 1), np.stack(r, 0)[None]


def kernel(**inputs):
    import concourse.bacc as bacc
    from concourse.bass_utils import run_bass_kernel_spmd

    v = {k: np.asarray(a) for k, a in inputs.items()}
    w, c, r = laid_out(v)
    k32, k16 = constants()
    k16 = k16.astype(mybir.dt.np(BF16))
    arrays = {"x": v["x"], "ctx": v["ctx_1024"], "weights": w, "columns": c, "rows": r, "const32": k32, "const16": k16}
    arrays = {n: np.ascontiguousarray(a) for n, a in arrays.items()}

    def build(known):
        nc = bacc.Bacc("TRN2", target_bir_lowering=False, num_devices=1)
        args = [nc.dram_tensor(n, a.shape, BF16 if n == "const16" else F32, kind="ExternalInput").ap()
                for n, a in arrays.items()]
        out = nc.dram_tensor("out", (SEQS, S, D), F32, kind="ExternalOutput").ap()
        return nc, network(nc, *args, out, known)

    _, known = build(None)
    nc, _ = build(known)
    result = run_bass_kernel_spmd(nc, [arrays], core_ids=[0])
    return result.results[0]["out"]
```

```python
from contextlib import ExitStack

import numpy as np

import concourse.bass as bass
from concourse import mybir

F32 = mybir.dt.float32
BF16 = mybir.dt.bfloat16
ACT = mybir.ActivationFunctionType
ALU = mybir.AluOpType
AX = mybir.AxisListType

P = 128
SEQS, S, D = 64, 64, 128
STREAMS = 4
NB = 4
NT = NB // 2
TOK = NB * S
GROUPS = SEQS // (STREAMS * NB)
BIG = 1.0e30
ABSENT = 4294967296.0 * 32.0 ** 0.5

ATTS = range(8)
PAIRS = [8, 8, 8, 8, 8, 2, 2, 2]
CAUSAL = [True, False, False, True, False, False, False, False]
KEYMASK = ["length", "length", None, None, None, "sum", "sum", "sum"]
QUERYMASK = [True, True, False, False, False, True, True, True]
KV_FROM = ["xf", "kf", "kf", "xf", "cf", "cf", "xf", "xf"]
BETWEEN = [
    ("ctx _ _ x qm _ pv pq qs Qpar _ | "
     "pk Kpar qpair0 Kpair qpair1 qpair2 qpair3 _ first nz length lm | "
     "maskrow lrow A0 mx0 _ A1 mx1 _ nm maxrow mrow _"),
    ("_ O sum n1 _ x1 _ nkv kv pq qs | "
     "Qpar pk Kpar Kpair qpair0 qpair1 qpair2 qpair3 _ first nz pv length lm | "
     "maskrow lrow A0 mx0 A1 mx1 nm maxrow mrow _"),
    ("O sum _ n1 x1 _ fc1 fc2 | "
     "z _ n3 _ nq q kvstats nkv kv pq _ qs Qpar pk Kpar _ Kpair | "
     "qpair0 qpair1 pv qpair2 qpair3 A0 mx0 A1 _ mx1 nm maxrow _ mrow"),
    ("O _ o wo addwo x up0 silu0 up1 silu1 up2 up3 | "
     "silu2 silu3 down addff nq q pq qs Qpar pk qpair0 | "
     "Kpar Kpair qpair1 pv qpair2 qpair3 A0 mx0 A1 mx1 nm maxrow mrow _ _"),
    ("_ O o wo addwo _ nq q _ _ pq qs | "
     "_ Qpar pk Kpar pv qpair0 qpair1 Kpair | "
     "qpair2 qpair3 A0 A1 mx0 mx1 _ _ nm _ maxrow _ _ mrow"),
    ("O o wo addwo nq q up0 | "
     "up1 up2 up3 down addff x qm pq qs Qpar pk Kpar _ | "
     "qpair0 Kpair pv ksum km qpair1 maskrow lrow A0 mx0 nm maxrow mrow"),
    ("O sum n1 x1 ff leaky x | "
     "qm _ pq qs pk qpair0 Kpair Kpar qpair1 Qpar ksum pv _ km | "
     "maskrow lrow A0 mx0 nm maxrow mrow"),
    ("O sum _ n1 x1 ff _ leaky | "
     "x _ qm pq qs Qpar pk Kpar Kpair qpair0 ksum | "
     "qpair1 pv km maskrow lrow A0 mx0 _ nm maxrow mrow _"),
    ("O sum _ _ | "
     "n1 x1 | "
     "ff leaky"),
]


def stretches(a):
    return [lot.split() for lot in BETWEEN[a].split("|")]


WEIGHTS = (["wq0", "wk0", "wv0", "wq1", "wk1", "wv1", "fc1", "fc2", "wq2", "wk2", "wv2", "wo2"]
           + [f"u2_{c}" for c in range(4)] + [f"d2_{c}" for c in range(4)]
           + ["wq3", "wk3", "wv3", "wo3", "wq4", "wk4", "wv4", "wo4"]
           + [f"u4_{c}" for c in range(4)] + [f"d4_{c}" for c in range(4)]
           + [f"{w}{a}" for a in (5, 6, 7) for w in ("wq", "wk", "wv", "ff")])
COLUMNS = (["fc1_b", "q2_g", "q2_b", "kv2_g", "kv2_b"] + [f"u2_b{c}" for c in range(4)]
           + ["q3_g", "q3_b", "q4_g", "q4_b", "q5_g", "q5_b"] + [f"u4_b{c}" for c in range(4)]
           + ["bq5", "bq6", "bq7", "bk5", "bk6", "bk7"])
ROWS = ["n1_g", "n1_b", "n2_g", "n2_b", "n3_g", "n3_b", "fc2_b", "bo2", "d2_b", "d4_b",
        "e6_g", "e7_g", "e8_g", "e6_b", "e7_b", "e8_b", "bv5", "bv6", "bv7", "bff6", "bff7", "bff8"]
SPLIT = ROWS[-6:]
CONST32 = [("ident", 128), ("pair8", 8), ("pair2", 2), ("par8", 2), ("par2", 2), ("pos", 1),
           ("own8", 8), ("own2", 2 * NB), ("half", 2)]
CONST16 = [("identb", 128), ("fold", 64), ("sel8", NB * 128), ("sel2", 128), ("onesb", 128), ("samepar", 128), ("samekey", 128),
           ("causB", 64), ("causA", 64), ("pairb8", 8 * S), ("pairb2", 2 * S)]


def constants():
    p = np.arange(P)
    eye = np.eye(P)
    c = {"ident": eye, "identb": eye, "onesb": np.ones((P, 128)), "pos": (p % S)[:, None]}
    for n, pairs in (("8", 8), ("2", 2)):
        dh = D // (2 * pairs)
        c["pair" + n] = (p // (2 * dh))[:, None] == np.arange(pairs)
        c["pairb" + n] = np.repeat(c["pair" + n], S, axis=1)
        c["par" + n] = (p // dh % 2)[:, None] == np.arange(2)
    c["fold"] = (p % S)[:, None] == np.arange(S)
    parity = np.arange(P) // S
    c["own8"] = (p % 8)[:, None] == np.arange(8)
    c["sel8"] = ((p // 16)[:, None, None] == np.arange(NB)[None, :, None]) & \
        ((p // 8 % 2)[:, None, None] == parity[None, None, :])
    c["sel8"] = np.where((p < 16 * NB)[:, None, None], c["sel8"],
                         (p % S)[:, None, None] == (p % S)[None, None, :])
    c["own2"] = ((p // 4)[:, None, None] == np.arange(NB)[None, :, None]) & ((p % 2)[:, None, None] == np.arange(2))
    c["sel2"] = (p // 2 % 2)[:, None] == parity[None, :]
    c["half"] = parity[:, None] == np.arange(2)
    c["samekey"] = (p % S)[:, None] == (p % S)[None, :]
    c["samepar"] = parity[:, None] == parity[None, :]
    c["causB"] = -BIG * ((p % S)[:, None] > np.arange(S)[None, :])
    c["causA"] = -BIG * (np.arange(S)[None, :] > (p % S)[:, None])
    flat = lambda names: np.concatenate([np.reshape(c[n], (P, w)).astype(np.float32) for n, w in names], 1)
    return flat(CONST32), flat(CONST16)


class Section:

    def __init__(self, known):
        self.known = known
        self.counts = {"signals": {}, "filled": {}, "readers": {}}
        self.place = 0


class Signal:

    def __init__(self, ctx, nc, name):
        self.sem, self.name = ctx.enter_context(nc.semaphore(name)), name

    def start(self, section):
        self.section, self.count = section, 0
        self.events = section.counts["signals"][self.name] = {}

    def mark(self, *event, by=1, place=None):
        self.count += by
        self.events[event] = self.count, self.section.place if place is None else place
        return self.sem, by

    def at(self, *event):
        if not self.section.known:
            return self.sem, 0
        count, place = self.section.known["signals"][self.name][event]
        return self.sem, count if place <= self.section.place else 0


class Banks:

    def __init__(self, ctx, nc):
        self.filled = [ctx.enter_context(nc.semaphore(f"filled{k}")) for k in range(8)]
        self.tensor = [ctx.enter_context(nc.psum_tensor(f"bank{k}", [P, 512], F32)) for k in range(8)]

    def start(self, section):
        self.section, self.uses, self.last, self.turn = section, [0] * 8, {}, {}
        self.readers = section.counts["readers"]

    def take(self, pe, ring, *use):
        n = self.turn[ring] = self.turn.get(ring, -1) + 1
        k = ring[n % len(ring)]
        if self.section.known and k in self.last:
            for sem, count in self.section.known["readers"][self.last[k]].items():
                pe.wait_ge(self.sems[sem], count)
        self.last[k] = use
        self.uses[k] += 1
        self.section.counts["filled"][use] = k, self.uses[k], self.section.place
        return self.tensor[k]

    def full(self, *use):
        return self.filled[self.section.counts["filled"][use][0]], 1

    def of(self, *use):
        return self.tensor[self.section.known["filled"][use][0] if self.section.known else 0]

    def ready(self, *use):
        if not self.section.known:
            return self.filled[0], 0
        k, n, place = self.section.known["filled"][use]
        return self.filled[k], n if place <= self.section.place else 0

    def drain(self, use, signal, *event):
        if self.section.known:
            assert self.section.known["filled"][use][2] <= self.section.place, use
        sem, by = signal.mark(*event)
        self.readers.setdefault(use, {})[signal.name] = signal.count
        return sem, by


NPT = 4
RING_S = (0, 1, 2, 3)
RING_O = (4,)
RING_M = (5, 6, 7)


def network(nc, x, ctx_in, weights, columns, rows, const32, const16, out, known):
    x_g = x.rearrange("(i s j p) t d -> i s (p t) j d", i=GROUPS, s=STREAMS, p=2)
    c_g = ctx_in.rearrange("(i s j p) t d -> i s (p t) j d", i=GROUPS, s=STREAMS, p=2)
    o_g = out.rearrange("(i s j p) t d -> i s (p t) j d", i=GROUPS, s=STREAMS, p=2)

    with ExitStack() as ctx:
        def sb(name, shape, dt=F32):
            return ctx.enter_context(nc.sbuf_tensor(name, shape, dt))

        def per_stream(name, shape, dt=F32):
            return [sb(f"{name}{s}", shape, dt) for s in range(STREAMS)]

        W_all = sb("W_all", [P, len(WEIGHTS), 128])
        cols = sb("cols", [P, len(COLUMNS)])
        half = sb("half", [P, 4])
        bkpar = sb("bkpar", [P, 3, 2])
        row = sb("row", [P, len(ROWS), 128])
        split = sb("split", [3, len(SPLIT), 128], BF16)
        c32 = sb("c32", [P, sum(w for _, w in CONST32)])
        c16 = sb("c16", [P, sum(w for _, w in CONST16)], BF16)

        def pick(buf, names, name):
            at = 0
            for n, w in names:
                if n == name:
                    return buf[:, at:at + w]
                at += w
            raise KeyError(name)

        def W(name):
            return W_all[:, WEIGHTS.index(name), :]

        def col(name):
            i = COLUMNS.index(name)
            return cols[:, i:i + 1]

        def rowb(name):
            return row[:, ROWS.index(name), :]

        def parts(name):
            return split[:, SPLIT.index(name), :]

        def K32(name):
            return pick(c32, CONST32, name)

        def K16(name):
            return pick(c16, CONST16, name)

        Xin = per_stream("Xin", [P, NT, 128])
        C = per_stream("C", [P, NT, 128])
        X = per_stream("X", [P, NT, 128])
        Y = per_stream("Y", [P, NT, 128])
        Y2 = per_stream("Y2", [P, NT, 128])
        O = per_stream("O", [P, NT, 128])
        xf = per_stream("xf", [P, TOK])
        kf = per_stream("kf", [P, TOK])
        cf = per_stream("cf", [P, TOK])
        of = kf
        hid = per_stream("hid", [P, 4, TOK])
        tnh = per_stream("tnh", [P, 2, TOK])
        qs = per_stream("qs", [P, TOK])
        qb = per_stream("qb", [P, TOK], BF16)
        kb = per_stream("kb", [P, TOK], BF16)
        Qpar = per_stream("Qpar", [P, NB, 2, S], BF16)
        Kpar = per_stream("Kpar", [P, NB, 2, S])
        Qpair = per_stream("Qpair", [P, NB * 8 * S])
        Kpair = per_stream("Kpair", [P, NB * 8 * S], BF16)
        V8 = per_stream("V8", [P, NB, 8, 2, 9])
        V2 = per_stream("V2", [P, NB, 2, 2, 33])
        mx = per_stream("mx", [P, NB * 8])
        nm8 = per_stream("nm8", [P, NB, 2, 8], BF16)
        nm2 = per_stream("nm2", [P, NB, 2, 2], BF16)
        lm8 = per_stream("lm8", [P, NB, 2, 8], BF16)
        lm2 = per_stream("lm2", [P, NB, 2, 2], BF16)
        mrow = per_stream("mrow", [P, 512], BF16)
        lrow = per_stream("lrow", [P, 512], BF16)
        nz = per_stream("nz", [P, NB * 8], BF16)
        km = per_stream("km", [P, NB * 8], BF16)
        kz = per_stream("kz", [P, NB], BF16)
        ac = per_stream("ac", [P, NT])
        rd = per_stream("rd", [P, NT, 16])
        rq = per_stream("rq", [P, NT, 16])
        stats = per_stream("stats", [P, NT, 6])
        mv = per_stream("mv", [P, NT, 2])
        rstd = per_stream("rstd", [P, NT])
        ve = per_stream("ve", [P, NT])
        dev = per_stream("dev", [P, NT])
        am = per_stream("am", [P, NT])
        m0 = per_stream("m0", [P, NT])
        qm = per_stream("qm", [P, NT])
        PT = sb("PT", [P, NPT, 512])
        expo = sb("expo", [P, 3, NT])

        banks = Banks(ctx, nc)
        signals = {}

        def sig(name):
            if name not in signals:
                signals[name] = Signal(ctx, nc, name)
            return signals[name]

        setup = ctx.enter_context(nc.semaphore("setup"))
        setdve = ctx.enter_context(nc.semaphore("setdve"))
        loaded_w = ctx.enter_context(nc.semaphore("loaded_w"))

        x_in = [sig(f"x_in{s}") for s in range(STREAMS)]
        c_in = [sig(f"c_in{s}") for s in range(STREAMS)]
        x_out = [sig(f"x_out{s}") for s in range(STREAMS)]
        operand = sig("operand")
        probs = sig("probs")
        vec = sig("vec")
        pool = sig("pool")
        banks.sems = {n: signals[n].sem for n in signals}

        with nc.Block() as block:
            @block.sync
            def _(sp):
                sp.dma_start(c32[:], const32).then_inc(loaded_w, 16)
                sp.dma_start(c16[:], const16).then_inc(loaded_w, 16)
                sp.dma_start(cols[:], columns).then_inc(loaded_w, 16)
                sp.dma_start(W_all[:], weights.rearrange("p (n c) -> p n c", c=128)).then_inc(loaded_w, 16)
                sp.dma_start(row[:], rows.broadcast_to((P, len(ROWS), 128))).then_inc(loaded_w, 16)
                sp.wait_ge(loaded_w, 80)

            @block.gpsimd
            def _(g):
                n = 0
                for s in range(STREAMS):
                    for buf in (nm8, nm2, lm8, lm2, V8, V2):
                        g.memset(buf[s][:], 0.0).then_inc(setup, 1)
                        n += 1
                g.memset(expo[:, 0, :], -0.5).then_inc(setup, 1)
                g.memset(expo[:, 1, :], 0.5).then_inc(setup, 1)
                g.memset(expo[:, 2, :], -1.0).then_inc(setup, 1)
                g.wait_ge(setup, n + 3)
                for s in range(STREAMS):
                    for par in range(2):
                        rows_ = slice(64 * par, 64 * par + 64)
                        g.memset(V8[s][rows_, :, :, par, 8:9], 1.0).then_inc(setup, 1)
                        g.memset(V2[s][rows_, :, :, par, 32:33], 1.0).then_inc(setup, 1)
                g.wait_ge(setup, n + 3 + 4 * STREAMS)

            @block.vector
            def _(v):
                v.wait_ge(loaded_w, 80)
                i = COLUMNS.index("u2_b0")
                v.tensor_scalar(half[:], cols[:, i:i + 4], 0.5, None, ALU.mult).then_inc(setdve, 1)
                for i in range(3):
                    v.tensor_scalar(bkpar[:, i, :], K32("par2"), col(f"bk{5 + i}"), None, ALU.mult
                                    ).then_inc(setdve, 1)
                for s in range(STREAMS):
                    for spread, mask in ((mrow, "causB"), (lrow, "causA")):
                        rows_ = slice(16 * NB, P)
                        v.tensor_copy(spread[s][rows_, :].rearrange("p (h t) -> p h t", t=S),
                                      K16(mask)[rows_, :].unsqueeze(1).broadcast_to((P - 16 * NB, 8, S))
                                      ).then_inc(setdve, 1)
                n = 4 + 2 * STREAMS
                size = len(SPLIT) * 128
                whole = row[0:3, len(ROWS) - len(SPLIT):, :].rearrange("p n c -> p (n c)")
                rest = hid[0].rearrange("p c t -> p (c t)")[0:3, 0:size]
                part = [Kpair[k][0:3, 0:size] for k in range(3)]
                v.tensor_copy(part[0], whole).then_inc(setdve, 1)
                v.wait_ge(setdve, n + 1)
                v.tensor_tensor(rest, whole, part[0], ALU.subtract).then_inc(setdve, 1)
                v.wait_ge(setdve, n + 2)
                v.tensor_copy(part[1], rest).then_inc(setdve, 1)
                v.wait_ge(setdve, n + 3)
                v.tensor_tensor(part[2], rest, part[1], ALU.subtract).then_inc(setdve, 1)
                sum_ = split[:].rearrange("p n c -> p (n c)")
                v.tensor_scalar(sum_, part[0], K32("ident")[0:3, 0:1], None, ALU.mult).then_inc(setdve, 1)
                for k in (1, 2):
                    v.wait_ge(setdve, n + 4 + k)
                    v.scalar_tensor_tensor(out=sum_, in0=part[k], scalar=K32("ident")[0:3, k:k + 1], in1=sum_,
                                           op0=ALU.mult, op1=ALU.add).then_inc(setdve, 1)
                v.wait_ge(setdve, n + 7)
        nc.all_engine_barrier()

        def unit(a):
            n = PAIRS[a] * S
            return NB * n // 512, 512 // n, n

        def units_of(name, a):
            units = unit(a)[0]
            return range(units)[2 * int(name[-1]):2 * int(name[-1]) + 2]

        def exp_number(a, s, u):
            return sum(STREAMS * unit(i)[0] for i in range(a)) + s * unit(a)[0] + u

        kv_of = lambda a, s: {"xf": xf, "kf": kf, "cf": cf}[KV_FROM[a]][s]

        def kv_event(a, s):
            if KV_FROM[a] == "cf":
                return "ctx", 0, s
            if KV_FROM[a] == "kf":
                return "kv", a, s
            return q_step(a), a, s

        def q_step(a):
            return {0: "x", 1: "x1", 2: "q", 3: "q", 4: "q", 5: "x", 6: "x", 7: "x"}[a]

        def build_section(name, first, group):
            section = Section(known and known[name])
            banks.start(section)
            for signal in signals.values():
                signal.start(section)

            def walk(loop_unit, step):
                for a in range(len(ATTS) if first else 0, len(ATTS) + 1):
                    for s in range(STREAMS):
                        section.place = STREAMS * a + s
                        todo = []
                        for ago in range(1, STREAMS):
                            other = (s - ago) % STREAMS
                            before = a + 1 if other < s else a
                            if before > len(ATTS):
                                before = 0
                            if not first or before == 0:
                                lot = stretches(before)[ago - 1]
                                todo += [((i + 0.5) / len(lot), ago, name, before, other) for i, name in enumerate(lot)]
                        todo.sort()
                        parts = unit(a)[0] + 1 if a in ATTS else 1
                        for u in range(parts):
                            if a in ATTS:
                                loop_unit(a, s, u)
                            for _, _, name, before, other in todo[u * len(todo) // parts:(u + 1) * len(todo) // parts]:
                                if name != "_":
                                    step(name, before, other)

            with nc.Block() as block:
                @block.sync
                def _(sp):
                    section.place = STREAMS * (len(ATTS) + 1)
                    coming = 0 if first else (group + 1) % GROUPS
                    for s in range(STREAMS):
                        if not first:
                            sp.wait_ge(*vec.at("sum", 1, s))
                        sp.dma_start(Xin[s][:], x_g[coming, s]).then_inc(*x_in[s].mark(by=16, place=STREAMS * len(ATTS)))
                        if not first:
                            sp.wait_ge(*vec.at("kv", 2, s))
                        sp.dma_start(C[s][:], c_g[coming, s]).then_inc(*c_in[s].mark(by=16, place=STREAMS * len(ATTS)))
                    if not first:
                        for s in range(STREAMS):
                            sp.wait_ge(*pool.at("enc", 8, s))
                            sp.dma_start(o_g[group, s], X[s][:]).then_inc(*x_out[s].mark(by=16))
                        for s in range(STREAMS):
                            sp.wait_ge(*x_out[s].at())
                    for s in range(STREAMS):
                        sp.wait_ge(*x_in[s].at())
                        sp.wait_ge(*c_in[s].at())

                @block.tensor
                def _(pe):
                    def turn(src, use):
                        t = banks.take(pe, RING_M, *use)
                        for j in range(NT):
                            mm = pe.transpose(t[:, 128 * j:128 * j + 128], src[:, j, :], K32("ident"))
                        mm.then_inc(*banks.full(*use))

                    def token_major(src, name, use):
                        t = banks.take(pe, RING_M, *use)
                        for j in range(NT):
                            mm = pe.matmul(t[:, 128 * j:128 * j + 128], src[:, 128 * j:128 * j + 128], W(name),
                                           start=True, stop=True)
                        mm.then_inc(*banks.full(*use))

                    def feature_major(src, name, use):
                        t = banks.take(pe, RING_M, *use)
                        pe.matmul(t[:, 0:TOK], W(name), src[:], start=True, stop=True).then_inc(*banks.full(*use))

                    def step(name, a, s):
                        use = (name, a, s)
                        if name == "ctx":
                            pe.wait_ge(*c_in[s].at())
                            turn(C[s], use)
                        elif name == "x":
                            if a == 0:
                                pe.wait_ge(*x_in[s].at())
                            elif a in (3, 5):
                                pe.wait_ge(*vec.at("wo" if a == 3 else "down", a, s))
                            else:
                                pe.wait_ge(*pool.at("enc", a, s))
                            turn(X[s] if a else Xin[s], use)
                        elif name == "x1":
                            pe.wait_ge(*vec.at("x1", a, s))
                            turn(X[s], use)
                        elif name == "q":
                            pe.wait_ge(*vec.at("q", a, s))
                            turn(Y[s], use)
                        elif name == "kv":
                            pe.wait_ge(*vec.at("kv", a, s))
                            turn(Y2[s], use)
                        elif name == "fc1":
                            pe.wait_ge(*operand.at("x1", a, s))
                            feature_major(xf[s], "fc1", use)
                        elif name == "fc2":
                            pe.wait_ge(*operand.at("fc1", a, s))
                            token_major(hid[s][:, 0, :], "fc2", use)
                        elif name == "o":
                            pe.wait_ge(*vec.at("O", a - 1, s))
                            turn(O[s], use)
                        elif name == "wo":
                            pe.wait_ge(*operand.at("o", a, s))
                            token_major(of[s], f"wo{a - 1}", use)
                        elif name[:2] == "up":
                            pe.wait_ge(*operand.at("x" if a == 3 else "q", a, s))
                            feature_major(xf[s], f"u{a - 1}_{name[2]}", use)
                        elif name == "down":
                            pe.wait_ge(*(vec if a == 3 else operand).at("up3", a, s))
                            t = banks.take(pe, RING_M, *use)
                            for j in range(NT):
                                for c in range(4):
                                    mm = pe.matmul(t[:, 128 * j:128 * j + 128], hid[s][:, c, 128 * j:128 * j + 128],
                                                   W(f"d{a - 1}_{c}"), start=c == 0, stop=c == 3)
                            mm.then_inc(*banks.full(*use))
                        elif name == "ff":
                            pe.wait_ge(*operand.at("x1", a, s))
                            t = banks.take(pe, RING_M, *use)
                            pe.matmul(t[:, 0:TOK], K16("onesb")[0:3, :],
                                      parts(f"bff{a}").unsqueeze(1).broadcast_to((3, NT, 128)),
                                      start=True, stop=False, skip_group_check=True)
                            for j in range(NT):
                                mm = pe.matmul(t[:, 128 * j:128 * j + 128], xf[s][:, 128 * j:128 * j + 128],
                                               W(f"ff{a - 1}"), start=False, stop=j == NT - 1, skip_group_check=True)
                            mm.then_inc(*banks.full(*use))
                        elif name == "pk":
                            pe.wait_ge(*operand.at(*kv_event(a, s)))
                            feature_major(kv_of(a, s), f"wk{a}", use)
                        elif name == "pq":
                            pe.wait_ge(*operand.at(q_step(a), a, s))
                            feature_major(xf[s], f"wq{a}", use)
                        elif name == "pv":
                            src, pairs = kv_of(a, s), PAIRS[a]
                            pe.wait_ge(*operand.at(*kv_event(a, s)))
                            t = banks.take(pe, RING_M, *use)
                            w = W(f"wv{a}").rearrange("p (h r d) -> p h r d", h=pairs, r=2)
                            if pairs == 2:
                                bias = parts(f"bv{a}").rearrange("p (h r d) -> p h r d", h=2, r=2)
                                for par in range(2):
                                    pe.matmul(t[64 * par:64 * par + 64, 0:TOK], K16("onesb")[0:3, 0:64],
                                              bias[:, :, par, :].unsqueeze(1).broadcast_to((3, NB, 2, 32)),
                                              start=True, stop=False, skip_group_check=True)
                            for b in range(NB):
                                for par in range(2):
                                    mm = pe.matmul(t[64 * par:64 * par + 64, S * b:S * b + S], src[:, S * b:S * b + S],
                                                   w[:, :, par, :], start=pairs == 8, stop=pairs == 8 or b == NB - 1,
                                                   skip_group_check=True)
                            mm.then_inc(*banks.full(*use))
                        elif name == "first":
                            pe.wait_ge(*operand.at(f"qpair{min(PAIRS[a], 4) - 1}", a, s))
                            pe.wait_ge(*operand.at("Kpar", a, s))
                            t = banks.take(pe, RING_M, *use)
                            q = Qpair[s].rearrange("p (b h q) -> p b h q", b=NB, q=S)
                            for b in range(NB):
                                mm = pe.matmul(t[:, 8 * b:8 * b + 8], Kpar[s][:, b].rearrange("p r t -> p (r t)"), q[:, b, :, 0],
                                               start=True, stop=True)
                            mm.then_inc(*banks.full(*use))
                        elif name == "length":
                            pe.wait_ge(*vec.at("nz", a, s))
                            t = banks.take(pe, RING_M, *use)
                            pe.matmul(t[:, 0:NB * 8], K16("samepar"), nz[s][:], start=True, stop=True
                                      ).then_inc(*banks.full(*use))
                        elif name == "ksum":
                            pe.wait_ge(*vec.at("kz", a, s))
                            t = banks.take(pe, RING_M, *use)
                            pe.matmul(t[:, 0:NB], K16("samekey"), kz[s][:], start=True, stop=True
                                      ).then_inc(*banks.full(*use))
                        elif name in ("maskrow", "maxrow"):
                            pe.wait_ge(*vec.at("lm" if name == "maskrow" else "nm", a, s))
                            t = banks.take(pe, RING_M, *use)
                            m = {("maskrow", 8): lm8, ("maskrow", 2): lm2, ("maxrow", 8): nm8, ("maxrow", 2): nm2}[
                                name, PAIRS[a]][s]
                            n = NB * 2 * PAIRS[a]
                            pe.matmul(t[0:n, 0:S], m.rearrange("p b r h -> p (b r h)"), K16("fold"),
                                      start=True, stop=True).then_inc(*banks.full(*use))
                        elif name in ("A0", "A1"):
                            pe.wait_ge(*vec.at("Kpair", a, s))
                            pe.wait_ge(*vec.at("Qpar", a, s))
                            if KEYMASK[a]:
                                pe.wait_ge(*vec.at("lrow", a, s))
                            for u in units_of(name, a):
                                scores("A", a, s, u, Qpar[s], Kpair[s])

                    def mask_terms(kind, a, s, u):
                        seqs, pairs = unit(a)[1], PAIRS[a]
                        terms = []
                        if kind == "A" and CAUSAL[a] and not KEYMASK[a]:
                            terms.append((K16("identb"), K16("causA").unsqueeze(1).broadcast_to((P, 8, S))))
                        if kind == "B" and KEYMASK[a]:
                            m = km[s][:, 8 * u:8 * u + 8]
                            terms.append((K16("identb"), m.unsqueeze(2).broadcast_to((P, 8, S))))
                        spread = [lrow] if kind == "A" and KEYMASK[a] else [mrow] if kind == "B" else []
                        for r in spread:
                            if pairs == 8:
                                n = P if CAUSAL[a] else 16 * NB
                                sel = K16("sel8").rearrange("p (b c) -> p b c", b=NB)[0:n, u, :]
                                terms.append((sel, r[s][0:n, :]))
                            else:
                                terms.append((K16("sel2")[0:4 * NB, :], r[s][0:4 * NB, :]))
                        return terms

                    def scores(kind, a, s, u, stationary, moving):
                        units, seqs, n = unit(a)
                        t = banks.take(pe, RING_S, kind, a, s, u)
                        terms = mask_terms(kind, a, s, u)
                        m = moving[:, 0:NB * n].rearrange("p (b c) -> p b c", b=NB)
                        for i in range(seqs):
                            b = seqs * u + i
                            mm = pe.matmul(t[:, n * i:n * i + n], stationary[:, b].rearrange("p r t -> p (r t)"),
                                           m[:, b, :], start=i == 0,
                                           stop=i == seqs - 1 and not terms, skip_group_check=True)
                        for i, (fixed, spread) in enumerate(terms):
                            mm = pe.matmul(t[:], fixed, spread, start=False, stop=i == len(terms) - 1,
                                           skip_group_check=True)
                        mm.then_inc(*banks.full(kind, a, s, u))

                    def values(a, s, u):
                        units, seqs, n = unit(a)
                        pairs = PAIRS[a]
                        w = 2 * (D // (2 * pairs) + 1)
                        V = (V8 if pairs == 8 else V2)[s]
                        pe.wait_ge(*probs.at(a, s, u))
                        if u == 0:
                            pe.wait_ge(*operand.at("V", a, s))
                        p = PT[:, exp_number(a, s, u) % NPT, :].rearrange("p (b h q) -> p b h q", h=pairs, q=S)
                        for i in range(seqs):
                            b = seqs * u + i
                            if b == 0:
                                outputs[0] = banks.take(pe, RING_O, "O", a, s)
                            r = slice(64 * (b % 2), 64 * (b % 2) + 64)
                            for h in range(pairs):
                                at = w * (pairs * (b // 2) + h)
                                mm = pe.matmul(outputs[0][r, at:at + w], p[:, i, h, :],
                                               V[:, b, h].rearrange("p r d -> p (r d)"), start=True, stop=True)
                            if b == NB - 1:
                                mm.then_inc(*banks.full("O", a, s))

                    outputs = [None]

                    def loop_unit(a, s, u):
                        if u < unit(a)[0]:
                            if u == 0:
                                pe.wait_ge(*operand.at(f"qpair{min(PAIRS[a], 4) - 1}", a, s))
                                pe.wait_ge(*operand.at("Kpar", a, s))
                                pe.wait_ge(*vec.at("mrow", a, s))
                            scores("B", a, s, u, Kpar[s], Qpair[s])
                        if u >= 1:
                            values(a, s, u - 1)

                    walk(loop_unit, step)

                @block.scalar
                def _(act):
                    def move(dst, src, use, *event, f=ACT.Copy, **kw):
                        act.wait_ge(*banks.ready(*use))
                        act.activation(dst, src, f, **kw).then_inc(*banks.drain(use, operand, *event))

                    def step(name, a, s):
                        use = (name, a, s)
                        full = banks.of(*use)[:, 0:TOK] if name in (
                            "ctx", "x", "x1", "q", "kv", "fc1", "o", "ff", "pk", "pq", "pv", "up0", "up1", "up2", "up3"
                        ) else None
                        if name == "ctx":
                            move(cf[s][:], full, use, *use)
                        elif name in ("x", "x1"):
                            move(xf[s][:], full, use, *use)
                        elif name == "q":
                            move(xf[s][:], full, use, *use, f=ACT.Identity, scale=col(f"q{a}_g"), bias=col(f"q{a}_b"))
                        elif name == "kv" and a == 1:
                            move(kf[s][:], full, use, *use)
                        elif name == "kv":
                            move(kf[s][:], full, use, *use, f=ACT.Identity, scale=col("kv2_g"), bias=col("kv2_b"))
                        elif name == "fc1":
                            move(hid[s][:, 0, :], full, use, *use, f=ACT.Relu, bias=col("fc1_b"))
                        elif name == "o":
                            move(of[s][:], full, use, *use)
                        elif name[:2] == "up" and a == 3:
                            c = int(name[2])
                            if c >= 2:
                                act.wait_ge(*vec.at(f"up{c - 2}", a, s))
                            move(tnh[s][:, c % 2, :], full, use, "tanh", *use, f=ACT.Tanh, scale=0.5,
                                 bias=half[:, c:c + 1])
                            move(hid[s][:, c, :], full, use, *use, f=ACT.Identity, bias=col(f"u2_b{c}"))
                        elif name[:2] == "up":
                            move(hid[s][:, int(name[2]), :], full, use, *use, f=ACT.Relu, bias=col(f"u4_b{name[2]}"))
                        elif name == "ff":
                            move(Y[s].rearrange("p j c -> p (j c)"), full, use, "fifth", a, s, scale=0.2)
                        elif name == "pq":
                            kw = {"f": ACT.Relu, "bias": col(f"bq{a}")} if PAIRS[a] == 2 else {}
                            move(qb[s][:], full, use, *use, **kw)
                        elif name == "qs":
                            kw = {"f": ACT.Relu, "bias": col(f"bq{a}")} if PAIRS[a] == 2 else {}
                            move(qs[s][:], banks.of("pq", a, s)[:, 0:TOK], ("pq", a, s), *use, **kw)
                        elif name == "pk":
                            kw = {"f": ACT.Relu, "bias": col(f"bk{a}")} if PAIRS[a] == 2 else {}
                            move(kb[s][:], full, use, *use, **kw)
                        elif name == "Kpar":
                            for h in range(2):
                                kw = {"f": ACT.Relu, "bias": bkpar[:, a - 5, h:h + 1]} if PAIRS[a] == 2 else {}
                                move(Kpar[s][:, :, h, :], banks.of("pk", a, s)[:, 0:TOK].rearrange(
                                    "p (b t) -> p b t", b=NB), ("pk", a, s), *use,
                                     scale=K32(f"par{PAIRS[a]}")[:, h:h + 1], **kw)
                        elif name[:5] == "qpair":
                            pairs = PAIRS[a]
                            d = Qpair[s][:, 0:NB * pairs * S].rearrange("p (b h t) -> p b h t", b=NB, h=pairs)
                            some = pairs // min(pairs, 4)
                            act.wait_ge(*operand.at("qs", a, s))
                            for h in range(pairs)[some * int(name[5]):some * int(name[5]) + some]:
                                act.activation(d[:, :, h, :], qs[s].rearrange("p (b t) -> p b t", b=NB), ACT.Copy,
                                               scale=K32(f"pair{pairs}")[:, h:h + 1]).then_inc(*operand.mark(*use))
                        elif name == "pv":
                            pairs = PAIRS[a]
                            dh = D // (2 * pairs)
                            V = (V8 if pairs == 8 else V2)[s]
                            t = full.rearrange("p (b h d) -> p b h d", b=NB, h=pairs)
                            for par in range(2):
                                r = slice(64 * par, 64 * par + 64)
                                move(V[r, :, :, par, 0:dh], t[r], use, *(("V", a, s) if par else ("V0", a, s)),
                                     f=ACT.Relu if pairs == 2 else ACT.Copy)

                    def loop_unit(a, s, u):
                        if u == unit(a)[0]:
                            return
                        n = exp_number(a, s, u)
                        if n >= NPT:
                            act.wait_ge(*banks.ready("O", *exp_user[n - NPT]))
                        act.wait_ge(*banks.ready("B", a, s, u))
                        act.activation(PT[:, n % NPT, :], banks.of("B", a, s, u)[:], ACT.Exp,
                                       scale=float((D // (2 * PAIRS[a])) ** -0.5)
                                       ).then_inc(*banks.drain(("B", a, s, u), probs, a, s, u))

                    exp_user = {exp_number(a, s, u): (a, s)
                                for a in ATTS for s in range(STREAMS) for u in range(unit(a)[0])}
                    walk(loop_unit, step)

                @block.vector
                def _(dve):
                    def moments(src, *tag):
                        for j in range(NT):
                            dve.bn_stats(stats[tag[-1]][:, j, :], src[:, j, :]).then_inc(*vec.mark("stats", *tag))
                        dve.wait_ge(*vec.at("stats", *tag))
                        for j in range(NT):
                            dve.bn_aggr(mv[tag[-1]][:, j, :], stats[tag[-1]][:, j, :]).then_inc(*vec.mark("mv", *tag))

                    def norm(dst, src, *tag):
                        s = tag[-1]
                        dve.wait_ge(*pool.at("rstd", *tag))
                        for j in range(NT):
                            dve.tensor_scalar(dst[:, j, :], src[:, j, :], mv[s][:, j, 0:1], rstd[s][:, j:j + 1],
                                              ALU.subtract, ALU.mult).then_inc(*vec.mark(*tag))

                    def norm_affine(name, *tag):
                        s = tag[-1]
                        dve.wait_ge(*vec.at("mv", *tag))
                        for j in range(NT):
                            dve.scalar_tensor_tensor(out=Y[s][:, j, :], in0=X[s][:, j, :], scalar=mv[s][:, j, 0:1],
                                                     in1=rowb(name + "_g"), op0=ALU.subtract, op1=ALU.mult
                                                     ).then_inc(*vec.mark("scaled", *tag))
                        dve.wait_ge(*vec.at("scaled", *tag))
                        dve.wait_ge(*pool.at("rstd", *tag))
                        for j in range(NT):
                            dve.scalar_tensor_tensor(out=X[s][:, j, :], in0=Y[s][:, j, :], scalar=rstd[s][:, j:j + 1],
                                                     in1=rowb(name + "_b"), op0=ALU.mult, op1=ALU.add
                                                     ).then_inc(*vec.mark(*tag))

                    def absent(sums, a, s):
                        dve.scalar_tensor_tensor(out=kz[s].rearrange("p (j r) -> p j r", r=2),
                                                 in0=sums[:].unsqueeze(2).broadcast_to((P, NT, 2)), scalar=0.0,
                                                 in1=K32("half").unsqueeze(1).broadcast_to((P, NT, 2)),
                                                 op0=ALU.is_equal, op1=ALU.mult).then_inc(*vec.mark("kz", a, s))

                    def present(a, s, op, absolute):
                        dve.tensor_reduce(am[s][:], (X if a else Xin)[s][:], AX.X, op, apply_absolute_value=absolute
                                          ).then_inc(*vec.mark("am", a, s))
                        dve.wait_ge(*vec.at("am", a, s))
                        dve.tensor_scalar(qm[s][:], am[s][:], 0.0, None, ALU.not_equal).then_inc(*vec.mark("qm", a, s))

                    def outputs(a, s):
                        heads = 2 * PAIRS[a]
                        dh = D // heads
                        t = banks.of("O", a, s)[:, 0:NT * heads * (dh + 1)].rearrange(
                            "p (j h d) -> p j h d", j=NT, h=heads)
                        dve.wait_ge(*banks.ready("O", a, s))
                        dve.reciprocal(rd[s][:, :, 0:heads], t[:, :, :, dh]).then_inc(*vec.mark("rd", a, s))
                        dve.wait_ge(*vec.at("rd", a, s))
                        f = rd
                        if QUERYMASK[a]:
                            dve.tensor_tensor(rq[s][:, :, 0:heads], rd[s][:, :, 0:heads],
                                              qm[s][:].unsqueeze(2).broadcast_to((P, NT, heads)), ALU.mult
                                              ).then_inc(*vec.mark("rq", a, s))
                            dve.wait_ge(*vec.at("rq", a, s))
                            f = rq
                        dve.tensor_tensor(O[s].rearrange("p j (h d) -> p j h d", h=heads), t[:, :, :, 0:dh],
                                          f[s][:, :, 0:heads].unsqueeze(3).broadcast_to((P, NT, heads, dh)),
                                          ALU.mult).then_inc(*banks.drain(("O", a, s), vec, "O", a, s))

                    def step(name, a, s):
                        use = (name, a, s)
                        r = [slice(0, 64), slice(64, 128)]
                        if name == "qm":
                            if a == 0:
                                dve.wait_ge(*x_in[s].at())
                                present(a, s, ALU.max, True)
                                dve.wait_ge(*vec.at("qm", a, s))
                                dve.tensor_copy(m0[s][:], qm[s][:]).then_inc(*vec.mark("m0", s))
                            else:
                                dve.wait_ge(*(vec.at("down", 5, s) if a == 5 else pool.at("enc", a, s)))
                                present(a, s, ALU.add, False)
                                if a > 5:
                                    absent(am[s], a, s)
                        elif name == "O":
                            outputs(a - 1, s)
                        elif name == "sum":
                            dve.wait_ge(*vec.at("O", a - 1, s))
                            dve.tensor_tensor(X[s][:], (Xin if a == 1 else X)[s][:], O[s][:], ALU.add).then_inc(*vec.mark("sum", a, s))
                            dve.wait_ge(*vec.at("sum", a, s))
                            moments(X[s], "x1", a, s)
                        elif name == "n1":
                            norm_affine(f"n{a}" if a < 3 else f"e{a}", "x1", a, s)
                            if a == 1:
                                dve.wait_ge(*vec.at("x1", a, s))
                                present(a, s, ALU.max, True)
                        elif name == "nkv" and a == 1:
                            dve.wait_ge(*vec.at("qm", a, s))
                            for j in range(NT):
                                dve.tensor_scalar(Y2[s][:, j, :], C[s][:, j, :], qm[s][:, j:j + 1], None, ALU.mult
                                                  ).then_inc(*vec.mark("kv", a, s))
                        elif name == "kvstats":
                            moments(C[s], "kv", a, s)
                            dve.tensor_reduce(ac[s][:], C[s][:], AX.X, ALU.add).then_inc(*vec.mark("ac", a, s))
                            dve.wait_ge(*vec.at("ac", a, s))
                            absent(ac[s], 5, s)
                        elif name == "nkv":
                            dve.wait_ge(*banks.ready("kv", 1, s))
                            norm(Y2[s], C[s], "kv", a, s)
                        elif name == "nq":
                            norm(Y[s], X[s], "q", a, s)
                        elif name == "z":
                            use = ("fc2", a, s)
                            dve.wait_ge(*banks.ready(*use))
                            dve.tensor_tensor(Y[s][:], banks.of(*use)[:, 0:TOK].rearrange("p (j c) -> p j c", j=NT),
                                              rowb("fc2_b").unsqueeze(1).broadcast_to((P, NT, 128)), ALU.add
                                              ).then_inc(*banks.drain(use, vec, "z", a, s))
                            dve.wait_ge(*vec.at("z", a, s))
                            for j in range(NT):
                                dve.scalar_tensor_tensor(out=X[s][:, j, :], in0=Y[s][:, j, :], scalar=m0[s][:, j:j + 1],
                                                         in1=X[s][:, j, :], op0=ALU.mult, op1=ALU.add
                                                         ).then_inc(*vec.mark("x2", a, s))
                            dve.wait_ge(*vec.at("x2", a, s))
                            moments(X[s], "n3", a, s)
                        elif name == "n3":
                            norm_affine("n3", "n3", a, s)
                            dve.wait_ge(*vec.at("n3", a, s))
                            moments(X[s], "q", a, s)
                        elif name in ("addwo", "addff"):
                            name = "wo" if name == "addwo" else "down"
                            use = (name, a, s)
                            if a == 3 or name == "down":
                                dve.wait_ge(*pool.at("bias", name, a, s))
                            dve.wait_ge(*banks.ready(*use))
                            dve.scalar_tensor_tensor(out=X[s].rearrange("p j c -> p (j c)"), in0=banks.of(*use)[:, 0:TOK],
                                                     scalar=0.5 if use[:2] == ("down", 3) else 1.0,
                                                     in1=X[s].rearrange("p j c -> p (j c)"), op0=ALU.mult, op1=ALU.add
                                                     ).then_inc(*banks.drain(use, vec, *use))
                            if (name, a) in (("down", 3), ("wo", 4), ("wo", 5)):
                                dve.wait_ge(*vec.at(*use))
                                moments(X[s], "q", a, s)
                        elif name == "leaky":
                            use = ("ff", a, s)
                            dve.wait_ge(*operand.at("fifth", a, s))
                            y = Y[s].rearrange("p j c -> p (j c)")
                            dve.scalar_tensor_tensor(out=y, in0=banks.of(*use)[:, 0:TOK], scalar=1.0, in1=y, op0=ALU.mult,
                                                     op1=ALU.max).then_inc(*banks.drain(use, vec, "leaky", a, s))
                        elif name[:4] == "silu":
                            c = int(name[4])
                            dve.wait_ge(*operand.at(f"up{c}", a, s))
                            dve.scalar_tensor_tensor(out=hid[s][:, c, :], in0=tnh[s][:, c % 2, :], scalar=1.0,
                                                     in1=hid[s][:, c, :], op0=ALU.add, op1=ALU.mult
                                                     ).then_inc(*vec.mark(f"up{c}", a, s))
                        elif name == "Qpar":
                            dve.wait_ge(*operand.at("pq", a, s))
                            for h in range(2):
                                dve.tensor_scalar(Qpar[s][:, :, h, :], qb[s].rearrange("p (b t) -> p b t", b=NB),
                                                  K32(f"par{PAIRS[a]}")[:, h:h + 1], None, ALU.mult
                                                  ).then_inc(*vec.mark("Qpar", a, s))
                        elif name == "Kpair":
                            pairs = PAIRS[a]
                            dve.wait_ge(*operand.at("pk", a, s))
                            dve.tensor_tensor(Kpair[s][:, 0:NB * pairs * S].rearrange("p (b h t) -> p b h t", b=NB, h=pairs),
                                              kb[s].rearrange("p (b t) -> p b t", b=NB).unsqueeze(2).broadcast_to(
                                                  (P, NB, pairs, S)),
                                              K16(f"pairb{pairs}").rearrange("p (h t) -> p h t", h=pairs).unsqueeze(1)
                                              .broadcast_to((P, NB, pairs, S)), ALU.mult
                                              ).then_inc(*vec.mark("Kpair", a, s))
                        elif name == "nz":
                            use = ("first", a, s)
                            dve.wait_ge(*banks.ready(*use))
                            dve.tensor_scalar(nz[s][:], banks.of(*use)[:, 0:8 * NB], 0.0, None, ALU.not_equal
                                              ).then_inc(*banks.drain(use, vec, "nz", a, s))
                        elif name == "lm":
                            use = ("length", a, s)
                            dve.wait_ge(*banks.ready(*use))
                            dve.tensor_scalar(km[s][:], banks.of(*use)[:, 0:8 * NB], K32("pos"), -BIG, ALU.is_le, ALU.mult
                                              ).then_inc(*banks.drain(use, vec, "km", a, s))
                            dve.wait_ge(*vec.at("km", a, s))
                            for h in range(2):
                                dve.tensor_copy(lm8[s][r[h], :, h, :], km[s][r[h], :].rearrange("p (b h) -> p b h", b=NB)
                                                ).then_inc(*vec.mark("lm", a, s))
                        elif name == "km":
                            use = ("ksum", a, s)
                            dve.wait_ge(*banks.ready(*use))
                            k = banks.of(*use)[:, 0:NB].unsqueeze(2).broadcast_to((P, NB, 2))
                            for h in range(2):
                                dve.tensor_scalar(lm2[s][r[h], :, h, :], k[r[h]], -ABSENT, None, ALU.mult
                                                  ).then_inc(*vec.mark("lm", a, s))
                            dve.tensor_scalar(km[s][:, 0:2 * NB].rearrange("p (b h) -> p b h", b=NB), k,
                                              -ABSENT, None, ALU.mult).then_inc(*banks.drain(use, vec, "km", a, s))
                        elif name == "nm":
                            pairs = PAIRS[a]
                            dve.wait_ge(*vec.at("mx", a, s))
                            for h in range(2):
                                dst = (nm8 if pairs == 8 else nm2)[s][r[h], :, h, :]
                                src = mx[s][r[h], 0:NB * pairs].rearrange("p (b h) -> p b h", b=NB)
                                dve.tensor_scalar(dst, src, -1.0, None, ALU.mult).then_inc(*vec.mark("nm", a, s))
                        elif name in ("lrow", "mrow"):
                            dst, done, use = (lrow, "lrow", ("maskrow", a, s)) if name == "lrow" else (
                                mrow, "mrow", ("maxrow", a, s))
                            dve.wait_ge(*banks.ready(*use))
                            n, m = (16 * NB, 8) if PAIRS[a] == 8 else (4 * NB, 2 * NB)
                            dve.tensor_tensor(dst[s][0:n, 0:m * S].rearrange("p (m t) -> p m t", m=m),
                                              banks.of(*use)[0:n, 0:S].unsqueeze(1).broadcast_to((n, m, S)),
                                              K32(f"own{PAIRS[a]}")[0:n, :].unsqueeze(2).broadcast_to(
                                                  (n, m, S)), ALU.mult).then_inc(*banks.drain(use, vec, done, a, s))
                        elif name in ("mx0", "mx1"):
                            for u in units_of(name, a):
                                dve.wait_ge(*banks.ready("A", a, s, u))
                                dve.tensor_reduce(mx[s][:, 8 * u:8 * u + 8],
                                                  banks.of("A", a, s, u)[:].rearrange("p (h t) -> p h t", t=S),
                                                  AX.X, ALU.max).then_inc(*banks.drain(("A", a, s, u), vec, "mx", a, s))

                    walk(lambda a, s, u: None, step)

                @block.gpsimd
                def _(g_):
                    def deviation(sample, *tag):
                        s = tag[-1]
                        g_.wait_ge(*vec.at("mv", *tag))
                        if not sample:
                            g_.tensor_scalar(ve[s][:], mv[s][:, :, 1], 1e-5, None, ALU.add).then_inc(*pool.mark("ve", *tag))
                            g_.wait_ge(*pool.at("ve", *tag))
                            g_.tensor_tensor(rstd[s][:], ve[s][:], expo[:, 0, :], ALU.pow
                                             ).then_inc(*pool.mark("rstd", *tag))
                            return
                        g_.tensor_scalar(ve[s][:], mv[s][:, :, 1], D / (D - 1.0), None, ALU.mult
                                         ).then_inc(*pool.mark("ve", *tag))
                        g_.wait_ge(*pool.at("ve", *tag))
                        g_.tensor_tensor(dev[s][:], ve[s][:], expo[:, 1, :], ALU.pow).then_inc(*pool.mark("dev", *tag))
                        g_.wait_ge(*pool.at("dev", *tag))
                        g_.tensor_scalar(ve[s][:], dev[s][:], 1e-8, None, ALU.add).then_inc(*pool.mark("deve", *tag))
                        g_.wait_ge(*pool.at("deve", *tag))
                        g_.tensor_tensor(rstd[s][:], ve[s][:], expo[:, 2, :], ALU.pow).then_inc(*pool.mark("rstd", *tag))

                    def add_bias(name, a, s):
                        g_.tensor_tensor(X[s][:], X[s][:], rowb({("wo", 3): "bo2", ("down", 3): "d2_b", ("down", 5): "d4_b"}[
                            name, a]).unsqueeze(1).broadcast_to((P, NT, 128)), ALU.add
                            ).then_inc(*pool.mark("bias", name, a, s))

                    def step(name, a, s):
                        if name == "sum":
                            deviation(a >= 6, "x1", a, s)
                        elif name == "z":
                            deviation(False, "n3", a, s)
                        elif name == "kvstats":
                            deviation(False, "kv", a, s)
                        elif name == "n3" or (name == "addwo" and a > 3) or (name == "addff" and a == 3):
                            deviation(False, "q", a, s)
                        elif name == "wo" and a == 3:
                            g_.wait_ge(*vec.at("q", 2, s))
                            add_bias(name, a, s)
                        elif name == "down":
                            g_.wait_ge(*(banks.ready("x", 3, s) if a == 3 else vec.at("q", a, s)))
                            add_bias(name, a, s)
                        elif name == "leaky":
                            g_.wait_ge(*vec.at("leaky", a, s))
                            g_.tensor_tensor(X[s][:], X[s][:], Y[s][:], ALU.add).then_inc(*pool.mark("enc", a, s))

                    walk(lambda a, s, u: None, step)

            nc.all_engine_barrier()
            nc.gpsimd.sem_clear(range(banks.filled[0].num, pool.sem.num + 1))
            nc.all_engine_barrier()
            return section.counts

        counts = {"first": build_section("first", True, 0)}
        with nc.Fori(0, GROUPS) as g:
            counts["group"] = build_section("group", False, g)
        return counts


def laid_out(v):
    L = "L%d_xattn_"
    heads = lambda w: w.transpose(1, 0, 2).reshape(D, D)
    down = lambda w: [w[128 * c:128 * c + 128] for c in range(4)]
    across = lambda w: [w[:, 128 * c:128 * c + 128] for c in range(4)]
    l0, l1, l2, l3 = ({k[len(L % i):]: a for k, a in v.items() if k.startswith(L % i)} for i in range(4))
    w = [heads(l0["Wq1"]), heads(l0["Wk1"]), heads(l0["Wv1"]), heads(l0["Wq2"]), heads(l0["Wk2"]), heads(l0["Wv2"]),
         l0["fc1_w"].T, l0["fc2_w"].T, l1["Wq"].T, l1["Wkv"][:D].T, l1["Wkv"][D:].T, l1["Wo"].T]
    w += across(l1["W1"].T) + down(l1["W2"].T)
    w += [l2["sa_w" + n] for n in "qkvo"] + [l2["ca_w" + n] for n in "qkvo"] + across(l2["ffn_w1"]) + down(l2["ffn_w2"])
    w += [l3[n][i] for i in range(3) for n in ("Wq", "Wk", "Wv", "Wff")]
    c = [l0["fc1_b"], l1["ln_q_g"], l1["ln_q_b"], l1["ln_kv_g"], l1["ln_kv_b"]] + list(l1["b1"].reshape(4, 128))
    c += [l2[f"ln{i}_{n}"] for i in (1, 2, 3) for n in "gb"] + list(l2["ffn_b1"].reshape(4, 128))
    c += list(l3["bq"]) + list(l3["bk"])
    r = [l0[f"ln{i}_{n}"] for i in (1, 2, 3) for n in "gb"] + [l0["fc2_b"], l1["bo"], l1["b2"], l2["ffn_b2"]]
    r += list(l3["gamma"]) + list(l3["beta"]) + list(l3["bv"]) + list(l3["bff"])
    return np.concatenate(w, 1), np.stack(c, 1), np.stack(r, 0)[None]


def kernel(**inputs):
    import concourse.bacc as bacc
    from concourse.bass_utils import run_bass_kernel_spmd

    v = {k: np.asarray(a) for k, a in inputs.items()}
    w, c, r = laid_out(v)
    k32, k16 = constants()
    k16 = k16.astype(mybir.dt.np(BF16))
    arrays = {"x": v["x"], "ctx": v["ctx_1024"], "weights": w, "columns": c, "rows": r, "const32": k32, "const16": k16}
    arrays = {n: np.ascontiguousarray(a) for n, a in arrays.items()}

    def build(known):
        nc = bacc.Bacc("TRN2", target_bir_lowering=False, num_devices=1)
        args = [nc.dram_tensor(n, a.shape, BF16 if n == "const16" else F32, kind="ExternalInput").ap()
                for n, a in arrays.items()]
        out = nc.dram_tensor("out", (SEQS, S, D), F32, kind="ExternalOutput").ap()
        return nc, network(nc, *args, out, known)

    _, known = build(None)
    nc, _ = build(known)
    result = run_bass_kernel_spmd(nc, [arrays], core_ids=[0])
    return result.results[0]["out"]
```
